# Optimizing a Trainium2 kernel written in Bass

```python
import numpy as np
import jax
import jax.numpy as jnp

def _softmax(x, axis=-1):
    return jax.nn.softmax(x, axis=axis)

def _gelu(x):
    return jax.nn.gelu(x, approximate=True)

def _silu(x):
    return jax.nn.silu(x)

def _sigmoid(x):
    return jax.nn.sigmoid(x)

def _layernorm(x, axis=-1, eps=1e-05):
    m = jnp.mean(x, axis=axis, keepdims=True)
    v = jnp.var(x, axis=axis, keepdims=True)
    return (x - m) / jnp.sqrt(v + eps)

def _scatter_add(tgt, idx, src, axis=0):
    return tgt.at[idx].add(src)

def _segment_sum(src, seg, n):
    return jax.ops.segment_sum(src, seg, n)
kernel_name = 'mk_macaron_d1_jaxref_r8_d7bac2'

def setup_inputs(seed: int=0):
    np.random.seed(seed)
    _w = jnp.asarray

    def _L0_attn_setup():
        import jax, jax.numpy as jnp
        import numpy as np
        EPS = 1e-05
        CHUNK = 64

        def _short_conv(x, w):
            K = w.shape[1]
            T = x.shape[1]
            xp = jnp.pad(x, ((0, 0), (K - 1, 0), (0, 0)))
            y = sum((xp[:, i:i + T, :] * w[:, i] for i in range(K)))
            return jax.nn.silu(y)

        def _l2norm(x):
            return x * jax.lax.rsqrt(jnp.sum(x * x, -1, keepdims=True) + 1e-06)

        def _forward(hidden_states, Wq, Wk, Wv, conv_q, conv_k, conv_v, Wf1, Wf2, Wb, A_log, dt_bias, Wg, bg, o_norm_w, Wo):
            B, T, _ = hidden_states.shape
            H = A_log.shape[0]
            x = hidden_states
            q = _short_conv(x @ Wq, conv_q)
            k = _short_conv(x @ Wk, conv_k)
            v = _short_conv(x @ Wv, conv_v)
            Dk = q.shape[-1] // H
            Dv = v.shape[-1] // H
            q = _l2norm(q.reshape(B, T, H, Dk))
            k = _l2norm(k.reshape(B, T, H, Dk))
            v = v.reshape(B, T, H, Dv)
            beta = jax.nn.sigmoid(x @ Wb)
            g = (x @ Wf1 @ Wf2).reshape(B, T, H, Dk)
            g = -jnp.exp(A_log)[:, None] * jax.nn.softplus(g + dt_bias.reshape(H, Dk))
            gexp = jnp.exp(g)
            scale = Dk ** (-0.5)

            def step(S, inp):
                q_t, k_t, v_t, ge_t, b_t = inp
                S = S * ge_t[..., None]
                kv = jnp.einsum('bhk,bhkv->bhv', k_t, S)
                upd = (v_t - kv) * b_t[..., None]
                S = S + jnp.einsum('bhk,bhv->bhkv', k_t, upd)
                o_t = jnp.einsum('bhk,bhkv->bhv', q_t, S) * scale
                return (S, o_t)

            @jax.checkpoint
            def chunk_fn(S, chunk):
                return jax.lax.scan(step, S, chunk)

            def tm(a):
                a = jnp.moveaxis(a, 1, 0)
                return a.reshape((T // CHUNK, CHUNK) + a.shape[1:])
            S0 = jnp.zeros((B, H, Dk, Dv), dtype=q.dtype)
            _, o = jax.lax.scan(chunk_fn, S0, (tm(q), tm(k), tm(v), tm(gexp), tm(beta)))
            o = jnp.moveaxis(o.reshape((T, B, H, Dv)), 0, 1)
            gate_o = (x @ Wg + bg).reshape(B, T, H, Dv)
            on = o * jax.lax.rsqrt(jnp.mean(o * o, -1, keepdims=True) + EPS) * o_norm_w
            on = on * jax.nn.silu(gate_o)
            return on.reshape(B, T, H * Dv) @ Wo
        key = jax.random.key(seed)
        ks = jax.random.split(key, 16)
        B, T, D = (2, 256, 256)
        H, Dk, Dv, K = (16, 128, 128, 4)
        n = jax.random.normal
        return {'hidden_states': n(ks[0], (B, T, D), jnp.float32), 'Wq': n(ks[1], (D, H * Dk), jnp.float32) * D ** (-0.5), 'Wk': n(ks[2], (D, H * Dk), jnp.float32) * D ** (-0.5), 'Wv': n(ks[3], (D, H * Dv), jnp.float32) * D ** (-0.5), 'conv_q': n(ks[4], (H * Dk, K), jnp.float32) * 0.5, 'conv_k': n(ks[5], (H * Dk, K), jnp.float32) * 0.5, 'conv_v': n(ks[6], (H * Dv, K), jnp.float32) * 0.5, 'Wf1': n(ks[7], (D, Dv), jnp.float32) * D ** (-0.5), 'Wf2': n(ks[8], (Dv, H * Dk), jnp.float32) * Dv ** (-0.5), 'Wb': n(ks[9], (D, H), jnp.float32) * D ** (-0.5), 'A_log': jnp.log(jax.random.uniform(ks[10], (H,), jnp.float32, 1.0, 16.0)), 'dt_bias': jnp.zeros((H * Dk,), jnp.float32), 'Wg': n(ks[11], (D, H * Dv), jnp.float32) * D ** (-0.5), 'bg': jnp.zeros((H * Dv,), jnp.float32), 'o_norm_w': jnp.ones((Dv,), jnp.float32), 'Wo': n(ks[12], (H * Dv, D), jnp.float32) * (H * Dv) ** (-0.5)}
    _L0_attn_in = _L0_attn_setup()

    def _L0_ffn_setup():
        import jax, jax.numpy as jnp
        import numpy as np
        B, S, H, I, E, F, K, R, TOPK = (1, 128, 256, 176, 64, 8, 8, 8, 6)
        ISH = 2 * I

        def _fused_linear(x, W, qa, qb, scale, w):
            out = x @ W.T
            a = jnp.einsum('th,krh->tkr', x, qa)
            b = jnp.einsum('tkr,khr->tkh', a, qb)
            mix = jnp.einsum('tkh,tk->th', b, w)
            return out + scale[None, :] * mix

        def _moe_forward(hidden_states, gate_weight, inv_mapping, mask_up_W, gate_W, gate_qa, gate_qb, gate_scale, up_W, up_qa, up_qb, up_scale, down_W, down_qa, down_qb, down_scale, sh_gate_W, sh_up_W, sh_down_W):
            b, s, h = hidden_states.shape
            x = hidden_states.reshape(-1, h)
            T = x.shape[0]
            scores = jax.nn.softmax(x @ gate_weight.T, axis=-1)
            topk_w, topk_idx = jax.lax.top_k(scores, TOPK)
            w_dense = jnp.zeros((T, E), x.dtype).at[jnp.arange(T)[:, None], topk_idx].add(topk_w)
            flat = w_dense[:, inv_mapping]
            scalar = flat.sum(-1)
            soft = jax.nn.softmax(jnp.where(flat == 0, -1000000000.0, flat), axis=-1)

            def expert(muW, gW, gqa, gqb, gs, uW, uqa, uqb, us, dW, dqa, dqb, ds, w):
                xe = x + w @ muW.T
                gate = jax.nn.silu(_fused_linear(xe, gW, gqa, gqb, gs, w))
                up = _fused_linear(xe, uW, uqa, uqb, us, w)
                return _fused_linear(gate * up, dW, dqa, dqb, ds, w)
            outs = jax.vmap(expert, in_axes=(0,) * 13 + (1,))(mask_up_W, gate_W, gate_qa, gate_qb, gate_scale, up_W, up_qa, up_qb, up_scale, down_W, down_qa, down_qb, down_scale, soft)
            y = jnp.einsum('fth,tf->th', outs, scalar).reshape(b, s, h)
            sh = jax.nn.silu(hidden_states @ sh_gate_W.T) * (hidden_states @ sh_up_W.T) @ sh_down_W.T
            return y + sh
        key = jax.random.key(seed)
        ks = jax.random.split(key, 20)
        g = lambda k, shape, s=0.02: jax.random.normal(k, shape, jnp.float32) * s
        return {'hidden_states': jax.random.normal(ks[0], (B, S, H), jnp.float32), 'gate_weight': g(ks[1], (E, H)), 'inv_mapping': jnp.arange(E, dtype=jnp.int32).reshape(F, K), 'mask_up_W': g(ks[2], (F, H, K)), 'gate_W': g(ks[3], (F, I, H)), 'gate_qa': g(ks[4], (F, K, R, H)), 'gate_qb': g(ks[5], (F, K, I, R)), 'gate_scale': jnp.full((F, I), 0.1, jnp.float32), 'up_W': g(ks[6], (F, I, H)), 'up_qa': g(ks[7], (F, K, R, H)), 'up_qb': g(ks[8], (F, K, I, R)), 'up_scale': jnp.full((F, I), 0.1, jnp.float32), 'down_W': g(ks[9], (F, H, I)), 'down_qa': g(ks[10], (F, K, R, I)), 'down_qb': g(ks[11], (F, K, H, R)), 'down_scale': jnp.full((F, H), 0.1, jnp.float32), 'sh_gate_W': g(ks[12], (ISH, H)), 'sh_up_W': g(ks[13], (ISH, H)), 'sh_down_W': g(ks[14], (H, ISH))}
    _L0_ffn_in = _L0_ffn_setup()
    _d = {'L0_attn_hidden_states': _L0_attn_in['hidden_states'], 'L0_attn_Wq': _L0_attn_in['Wq'], 'L0_attn_Wk': _L0_attn_in['Wk'], 'L0_attn_Wv': _L0_attn_in['Wv'], 'L0_attn_conv_q': _L0_attn_in['conv_q'], 'L0_attn_conv_k': _L0_attn_in['conv_k'], 'L0_attn_conv_v': _L0_attn_in['conv_v'], 'L0_attn_Wf1': _L0_attn_in['Wf1'], 'L0_attn_Wf2': _L0_attn_in['Wf2'], 'L0_attn_Wb': _L0_attn_in['Wb'], 'L0_attn_A_log': _L0_attn_in['A_log'], 'L0_attn_dt_bias': _L0_attn_in['dt_bias'], 'L0_attn_Wg': _L0_attn_in['Wg'], 'L0_attn_bg': _L0_attn_in['bg'], 'L0_attn_o_norm_w': _L0_attn_in['o_norm_w'], 'L0_attn_Wo': _L0_attn_in['Wo'], 'L0_ffn_gate_weight': _L0_ffn_in['gate_weight'], 'L0_ffn_inv_mapping': _L0_ffn_in['inv_mapping'], 'L0_ffn_mask_up_W': _L0_ffn_in['mask_up_W'], 'L0_ffn_gate_W': _L0_ffn_in['gate_W'], 'L0_ffn_gate_qa': _L0_ffn_in['gate_qa'], 'L0_ffn_gate_qb': _L0_ffn_in['gate_qb'], 'L0_ffn_gate_scale': _L0_ffn_in['gate_scale'], 'L0_ffn_up_W': _L0_ffn_in['up_W'], 'L0_ffn_up_qa': _L0_ffn_in['up_qa'], 'L0_ffn_up_qb': _L0_ffn_in['up_qb'], 'L0_ffn_up_scale': _L0_ffn_in['up_scale'], 'L0_ffn_down_W': _L0_ffn_in['down_W'], 'L0_ffn_down_qa': _L0_ffn_in['down_qa'], 'L0_ffn_down_qb': _L0_ffn_in['down_qb'], 'L0_ffn_down_scale': _L0_ffn_in['down_scale'], 'L0_ffn_sh_gate_W': _L0_ffn_in['sh_gate_W'], 'L0_ffn_sh_up_W': _L0_ffn_in['sh_up_W'], 'L0_ffn_sh_down_W': _L0_ffn_in['sh_down_W']}
    _x0 = _d['L0_attn_hidden_states']
    _d['L0_attn_hidden_states'] = jax.random.normal(jax.random.fold_in(jax.random.key(seed), 1), (4, 256, 256), dtype=_x0.dtype)
    del _x0
    return _d

def reference(L0_attn_hidden_states, L0_attn_Wq, L0_attn_Wk, L0_attn_Wv, L0_attn_conv_q, L0_attn_conv_k, L0_attn_conv_v, L0_attn_Wf1, L0_attn_Wf2, L0_attn_Wb, L0_attn_A_log, L0_attn_dt_bias, L0_attn_Wg, L0_attn_bg, L0_attn_o_norm_w, L0_attn_Wo, L0_ffn_gate_weight, L0_ffn_inv_mapping, L0_ffn_mask_up_W, L0_ffn_gate_W, L0_ffn_gate_qa, L0_ffn_gate_qb, L0_ffn_gate_scale, L0_ffn_up_W, L0_ffn_up_qa, L0_ffn_up_qb, L0_ffn_up_scale, L0_ffn_down_W, L0_ffn_down_qa, L0_ffn_down_qb, L0_ffn_down_scale, L0_ffn_sh_gate_W, L0_ffn_sh_up_W, L0_ffn_sh_down_W):

    def _L0_attn_ref(hidden_states, Wq, Wk, Wv, conv_q, conv_k, conv_v, Wf1, Wf2, Wb, A_log, dt_bias, Wg, bg, o_norm_w, Wo):
        import jax, jax.numpy as jnp
        import numpy as np
        EPS = 1e-05
        CHUNK = 64

        def _short_conv(x, w):
            K = w.shape[1]
            T = x.shape[1]
            xp = jnp.pad(x, ((0, 0), (K - 1, 0), (0, 0)))
            y = sum((xp[:, i:i + T, :] * w[:, i] for i in range(K)))
            return jax.nn.silu(y)

        def _l2norm(x):
            return x * jax.lax.rsqrt(jnp.sum(x * x, -1, keepdims=True) + 1e-06)

        def _forward(hidden_states, Wq, Wk, Wv, conv_q, conv_k, conv_v, Wf1, Wf2, Wb, A_log, dt_bias, Wg, bg, o_norm_w, Wo):
            B, T, _ = hidden_states.shape
            H = A_log.shape[0]
            x = hidden_states
            q = _short_conv(x @ Wq, conv_q)
            k = _short_conv(x @ Wk, conv_k)
            v = _short_conv(x @ Wv, conv_v)
            Dk = q.shape[-1] // H
            Dv = v.shape[-1] // H
            q = _l2norm(q.reshape(B, T, H, Dk))
            k = _l2norm(k.reshape(B, T, H, Dk))
            v = v.reshape(B, T, H, Dv)
            beta = jax.nn.sigmoid(x @ Wb)
            g = (x @ Wf1 @ Wf2).reshape(B, T, H, Dk)
            g = -jnp.exp(A_log)[:, None] * jax.nn.softplus(g + dt_bias.reshape(H, Dk))
            gexp = jnp.exp(g)
            scale = Dk ** (-0.5)

            def step(S, inp):
                q_t, k_t, v_t, ge_t, b_t = inp
                S = S * ge_t[..., None]
                kv = jnp.einsum('bhk,bhkv->bhv', k_t, S)
                upd = (v_t - kv) * b_t[..., None]
                S = S + jnp.einsum('bhk,bhv->bhkv', k_t, upd)
                o_t = jnp.einsum('bhk,bhkv->bhv', q_t, S) * scale
                return (S, o_t)

            @jax.checkpoint
            def chunk_fn(S, chunk):
                return jax.lax.scan(step, S, chunk)

            def tm(a):
                a = jnp.moveaxis(a, 1, 0)
                return a.reshape((T // CHUNK, CHUNK) + a.shape[1:])
            S0 = jnp.zeros((B, H, Dk, Dv), dtype=q.dtype)
            _, o = jax.lax.scan(chunk_fn, S0, (tm(q), tm(k), tm(v), tm(gexp), tm(beta)))
            o = jnp.moveaxis(o.reshape((T, B, H, Dv)), 0, 1)
            gate_o = (x @ Wg + bg).reshape(B, T, H, Dv)
            on = o * jax.lax.rsqrt(jnp.mean(o * o, -1, keepdims=True) + EPS) * o_norm_w
            on = on * jax.nn.silu(gate_o)
            return on.reshape(B, T, H * Dv) @ Wo
        return _forward(hidden_states, Wq, Wk, Wv, conv_q, conv_k, conv_v, Wf1, Wf2, Wb, A_log, dt_bias, Wg, bg, o_norm_w, Wo)

    def _L0_ffn_ref(hidden_states, gate_weight, inv_mapping, mask_up_W, gate_W, gate_qa, gate_qb, gate_scale, up_W, up_qa, up_qb, up_scale, down_W, down_qa, down_qb, down_scale, sh_gate_W, sh_up_W, sh_down_W):
        import jax, jax.numpy as jnp
        import numpy as np
        B, S, H, I, E, F, K, R, TOPK = (1, 128, 256, 176, 64, 8, 8, 8, 6)
        ISH = 2 * I

        def _fused_linear(x, W, qa, qb, scale, w):
            out = x @ W.T
            a = jnp.einsum('th,krh->tkr', x, qa)
            b = jnp.einsum('tkr,khr->tkh', a, qb)
            mix = jnp.einsum('tkh,tk->th', b, w)
            return out + scale[None, :] * mix

        def _moe_forward(hidden_states, gate_weight, inv_mapping, mask_up_W, gate_W, gate_qa, gate_qb, gate_scale, up_W, up_qa, up_qb, up_scale, down_W, down_qa, down_qb, down_scale, sh_gate_W, sh_up_W, sh_down_W):
            b, s, h = hidden_states.shape
            x = hidden_states.reshape(-1, h)
            T = x.shape[0]
            scores = jax.nn.softmax(x @ gate_weight.T, axis=-1)
            topk_w, topk_idx = jax.lax.top_k(scores, TOPK)
            w_dense = jnp.zeros((T, E), x.dtype).at[jnp.arange(T)[:, None], topk_idx].add(topk_w)
            flat = w_dense[:, inv_mapping]
            scalar = flat.sum(-1)
            soft = jax.nn.softmax(jnp.where(flat == 0, -1000000000.0, flat), axis=-1)

            def expert(muW, gW, gqa, gqb, gs, uW, uqa, uqb, us, dW, dqa, dqb, ds, w):
                xe = x + w @ muW.T
                gate = jax.nn.silu(_fused_linear(xe, gW, gqa, gqb, gs, w))
                up = _fused_linear(xe, uW, uqa, uqb, us, w)
                return _fused_linear(gate * up, dW, dqa, dqb, ds, w)
            outs = jax.vmap(expert, in_axes=(0,) * 13 + (1,))(mask_up_W, gate_W, gate_qa, gate_qb, gate_scale, up_W, up_qa, up_qb, up_scale, down_W, down_qa, down_qb, down_scale, soft)
            y = jnp.einsum('fth,tf->th', outs, scalar).reshape(b, s, h)
            sh = jax.nn.silu(hidden_states @ sh_gate_W.T) * (hidden_states @ sh_up_W.T) @ sh_down_W.T
            return y + sh
        return _moe_forward(hidden_states, gate_weight, inv_mapping, mask_up_W, gate_W, gate_qa, gate_qb, gate_scale, up_W, up_qa, up_qb, up_scale, down_W, down_qa, down_qb, down_scale, sh_gate_W, sh_up_W, sh_down_W)
    x = L0_attn_hidden_states
    x = x + 0.5 * _L0_ffn_ref(_layernorm(x, axis=-1), L0_ffn_gate_weight, L0_ffn_inv_mapping, L0_ffn_mask_up_W, L0_ffn_gate_W, L0_ffn_gate_qa, L0_ffn_gate_qb, L0_ffn_gate_scale, L0_ffn_up_W, L0_ffn_up_qa, L0_ffn_up_qb, L0_ffn_up_scale, L0_ffn_down_W, L0_ffn_down_qa, L0_ffn_down_qb, L0_ffn_down_scale, L0_ffn_sh_gate_W, L0_ffn_sh_up_W, L0_ffn_sh_down_W)
    x = x + _L0_attn_ref(_layernorm(x, axis=-1), L0_attn_Wq, L0_attn_Wk, L0_attn_Wv, L0_attn_conv_q, L0_attn_conv_k, L0_attn_conv_v, L0_attn_Wf1, L0_attn_Wf2, L0_attn_Wb, L0_attn_A_log, L0_attn_dt_bias, L0_attn_Wg, L0_attn_bg, L0_attn_o_norm_w, L0_attn_Wo)
    x = x + 0.5 * _L0_ffn_ref(_layernorm(x, axis=-1), L0_ffn_gate_weight, L0_ffn_inv_mapping, L0_ffn_mask_up_W, L0_ffn_gate_W, L0_ffn_gate_qa, L0_ffn_gate_qb, L0_ffn_gate_scale, L0_ffn_up_W, L0_ffn_up_qa, L0_ffn_up_qb, L0_ffn_up_scale, L0_ffn_down_W, L0_ffn_down_qa, L0_ffn_down_qb, L0_ffn_down_scale, L0_ffn_sh_gate_W, L0_ffn_sh_up_W, L0_ffn_sh_down_W)
    return x

_drawn_inputs = setup_inputs


def setup_inputs(seed=0):
    import zlib

    import numpy as np

    out = dict(_drawn_inputs(seed))
    spreads = {'L0_attn_dt_bias': (0.0, 0.8),
     'L0_attn_bg': (0.0, 0.285),
     'L0_attn_o_norm_w': (1.0, 0.2),
     'L0_ffn_gate_scale': (0.10000000149011612, 0.6),
     'L0_ffn_up_scale': (0.10000000149011612, 0.6),
     'L0_ffn_down_scale': (0.10000000149011612, 0.6)}
    factors = {'L0_ffn_gate_weight': 8.0,
     'L0_ffn_mask_up_W': 8.0,
     'L0_ffn_gate_W': 8.0,
     'L0_ffn_gate_qa': 8.0,
     'L0_ffn_gate_qb': 8.0,
     'L0_ffn_up_W': 8.0,
     'L0_ffn_up_qa': 8.0,
     'L0_ffn_up_qb': 8.0,
     'L0_ffn_down_W': 8.0,
     'L0_ffn_down_qa': 8.0,
     'L0_ffn_down_qb': 8.0,
     'L0_ffn_sh_gate_W': 3.003,
     'L0_ffn_sh_up_W': 2.943,
     'L0_ffn_sh_down_W': 2.94}
    for name, (base, spread) in spreads.items():
        noise = np.random.default_rng([zlib.crc32(name.encode()), seed]).standard_normal(out[name].shape)
        drawn = base * np.exp(spread * noise) if base else spread * noise
        out[name] = jnp.asarray(drawn.astype(out[name].dtype))
    for name, factor in factors.items():
        out[name] = (out[name] * factor).astype(out[name].dtype)
    return out
```

```python
import concourse.bass as bass
from concourse import mybir
from contextlib import ExitStack

P = 128
NSEQ, T, D = 4, 256, 256
NTOK = NSEQ * T
NT = NTOK // P
KT = D // P
H = 16
NE, F, K8, R = 64, 8, 8, 8
KR = K8 * R
I = 176
IR = I - P
ISH = 352
TOPK = 6
HALF = NTOK // 2
STEPS = 2 * F
ACCS = 2 * STEPS + 4
LEVELS = 7

C_GU, C_QA, C_QB, C_D1, C_D2, C_DQ, C_EW = 0, 768, 1024, 1408, 1664, 1920, 2176
C_KQV, C_F2, C_CONV, C_DT, C_AL, C_HW = 0, 768, 896, 908, 909, 910
C_G, C_WO, C_BG, C_ON, C_TW = 0, 256, 512, 513, 514

SLOTS = [["k0", "k1"], ["q0", "vt0"], ["q1"], ["v0", "vt1"], ["v1"], ["g0"], ["g1"],
         [], ["gt0", "gt1"], ["sk0", "sk1"], ["sq0", "sq1"], [], ["dg0", "dg1"], []]
TURN = [n for slot in SLOTS for n in slot]
OWN = [n for n in TURN if n[:-1] in ("vt", "gt")]
NEXT = [n for n in TURN if n not in OWN]
assert len(TURN) % 2 == 0 and len(NEXT) % 2 == 0


def macaron_kernel(nc, x, gate_wT, expert_w, expert_scale, route_w, shared_gu, shared_down,
                   inv_map, head_w, tail_w, wf1, wb, out):
    f32 = mybir.dt.float32
    i32 = mybir.dt.int32
    u32 = mybir.dt.uint32
    ALU = mybir.AluOpType
    ACT = mybir.ActivationFunctionType
    AX = mybir.AxisListType

    ctx = ExitStack()
    with ctx:
        def sb(name, shape, dt=f32):
            return ctx.enter_context(nc.sbuf_tensor(name, shape, dt))

        def sem(name):
            return ctx.enter_context(nc.semaphore(name))

        x_res = sb("x_res", [P, NT, D])
        xnT = sb("xnT", [P, KT, NTOK])
        ident = sb("ident", [P, P])
        ones = sb("ones", [P, P])
        masks = sb("masks", [P, LEVELS, 64])
        eps_ln = sb("eps_ln", [P, 1])
        eps_l2 = sb("eps_l2", [P, 1])
        onehot = sb("onehot", [NE, NE])
        gwT = sb("gwT", [P, KT, NE])
        stats = sb("stats", [P, NT, 6])
        mv = sb("mv", [P, NT, 2])
        lnv = sb("lnv", [P, 4, NT])

        ARENA = 47600
        arena = sb("arena", [P, ARENA])
        spot = [0]

        def carve(*shape, parts=P):
            n = 1
            for s in shape:
                n *= s
            v = arena[0:parts, spot[0]:spot[0] + n]
            spot[0] += n
            assert spot[0] <= ARENA, spot[0]
            if len(shape) == 2:
                v = v.rearrange("p (a b) -> p a b", a=shape[0])
            elif len(shape) == 3:
                v = v.rearrange("p (a b c) -> p a b c", a=shape[0], b=shape[1])
            elif len(shape) == 4:
                v = v.rearrange("p (a b c d) -> p a b c d", a=shape[0], b=shape[1], c=shape[2])
            return v

        xn = carve(NT, D)
        ew = [carve(C_EW) for _ in range(2)]
        es = [carve(640) for _ in range(2)]
        rw = [carve(384, parts=NE) for _ in range(2)]
        shw = carve(KT, 2 * ISH)
        shd = carve(3, D)
        sco = carve(NT, NE + 2)
        lgt = carve(NT, NE + 2)
        wd = carve(NT, NE)
        small = carve(8, NT * K8)
        top8 = carve(NT, 8)
        half_scal = carve(F * NT)
        flat = carve(NT * F, K8)
        soft = carve(NT * F, K8)
        wdT = carve(NTOK, parts=NE)
        softT = carve(NTOK, parts=NE)
        xe = [carve(KT, HALF) for _ in range(2)]
        wes = [carve(HALF) for _ in range(2)]
        aw = carve(HALF)
        sg0, sg2 = carve(HALF), carve(HALF)
        h1 = [carve(HALF) for _ in range(2)]
        h2 = [carve(HALF) for _ in range(2)]
        shs = [carve(HALF) for _ in range(3)]
        shh = [carve(HALF) for _ in range(3)]
        spot[0] = 0
        kq = carve(2, NT, P)
        hw = carve(C_HW)
        tw = carve(C_TW)
        wf1s = carve(KT, P)
        wbs = carve(KT, H)
        xfT = carve(NTOK)
        beta = carve(H, NT)
        ebeta = carve(NT, H)
        raw = carve(3, NSEQ, T + 3)
        acc = carve(3, NSEQ, T)
        kqs = carve(2, NTOK)
        vs = carve(NTOK)
        rn = carve(2, NTOK)
        zg, eg, ge = carve(NTOK), carve(NTOK), carve(NTOK)
        nega = carve(2)
        qk = carve(2, NTOK)
        prod = rn[:, 0, :]
        diag = carve(NT)
        kr = carve(NT, P)
        tot = [ge] + [carve(NT * P >> l) for l in range(1, LEVELS)]
        vw = carve(2, NT, P)
        aq = carve(NT, P)
        bt = [carve(NT, P) for _ in range(LEVELS)]
        pt = [carve(NT, P) for _ in range(LEVELS)]
        vtok = carve(NT, P)
        uu = carve(NT, P)
        krt = carve(NSEQ, P)
        state = carve(NSEQ, P)
        r1 = carve(NSEQ, P)
        oT = carve(NT, P)
        sqo = carve(NTOK)
        gate = carve(NT, P)

        pb = [ctx.enter_context(nc.psum_tensor(f"pb{i}", [P, 512], f32)) for i in range(8)]

        S = {n: sem(n) for n in (
            "x_in", "consts_in", "inv_in", "shared_in", "attn_in", "consts", "pid", "onehot_made",
            "pads_made", "zeros_pool", "zeros_dve",
            "ln_stats", "ln_mv", "ln_var", "ln_step", "ln_rs", "ln_rsqrt", "ln_xn", "ln_tr", "ln_ev",
            "rt_logits", "rt_shift", "rt_exp", "rt_wd", "rt_wdt_tr", "rt_wdt", "rt_flat", "rt_mshift",
            "rt_mexp", "rt_soft", "rt_soft_tr", "rt_softT", "rt_chain",
            "sh_gate", "sh_up", "sh_silu", "sh_h", "sh_out",
            "ew_in0", "ew_in1", "scaled", "x_full", "we_full", "we_ev", "xe_made", "a_made", "aw_made",
            "gu_full", "silu_done", "h_made", "da_full", "daw_made", "out_full", "out_acc",
            "ffn_over", "attn_over", "stored",
            "beta_full", "beta_exp", "beta_step", "beta_made", "xf_full", "xf_ev",
            "head_in", "tail_in", "pj_full", "pj_free", "conv_tap", "silu_head", "sq_head", "g_step",
            "ea_made", "na_made", "sp_made", "ge_made", "rn_ln", "rn_made", "qk_made", "prod_made",
            "kr_set", "vw_set", "aq_set", "lvl_upd", "tot_made",
            "al_full", "masked", "p_full", "p_ev", "d_full", "vw_upd",
            "u0_full", "u0_ev", "krt_full", "krt_ev", "s_full", "s_ev", "o0_full", "o0_ev",
            "ks_full", "r1_made", "u1_full", "u1_ev", "o1_full", "o1_ev", "sqo_made", "n_full",
            "n_ln", "rno_made", "gm_made", "on_made", "wo_full", "wo_acc")}
        EW_IN = [S["ew_in0"], S["ew_in1"]]

        def halves(ap, m, s):
            return ap.rearrange("p (n s m) -> p n s m", s=2, m=m)[:, :, s, :]

        def turn_base(h):
            return len(TURN) * h + len(NEXT)

        def own(name, h, last):
            return len(TURN) * h + (len(NEXT) + (OWN if last else TURN).index(name) + 1)

        T0, T1 = 4, 7

        block = ctx.enter_context(nc.Block())

        @block.sync
        def _(sp):
            sp.dma_start(x_res[:, 0:4, :], x[0:4].rearrange("n p d -> p n d")).then_inc(S["x_in"], 16)
            sp.dma_start(x_res[:, 4:8, :], x[4:8].rearrange("n p d -> p n d")).then_inc(S["x_in"], 16)
            sp.dma_start(gwT[:, :, :], gate_wT).then_inc(S["consts_in"], 16)
            sp.dma_start(small[0:NE, 0, :].bitcast(i32), inv_map.partition_broadcast(NE)).then_inc(S["inv_in"], 16)

            def ffn(q):
                def group(f, pf):
                    sp.dma_start(rw[pf], route_w[f]).then_inc(EW_IN[pf], 16)
                    sp.dma_start(ew[pf], expert_w[f]).then_inc(EW_IN[pf], 16)
                    sp.dma_start(es[pf], expert_scale[f].partition_broadcast(P)).then_inc(EW_IN[pf], 16)

                sp.dma_start(shw, shared_gu).then_inc(S["shared_in"], 16)
                sp.dma_start(shd, shared_down).then_inc(S["shared_in"], 16)
                for f in range(2):
                    group(f, f)
                with sp.Fori(0, F // 2 - 1) as i:
                    for pf in range(2):
                        sp.wait_ge(S["out_full"], 8 * i + (2 * STEPS * q + 4 * (pf + 1)))
                        group(bass.ds(2 * i + (2 + pf), 1), pf)

            ffn(0)
            sp.wait_ge(S["ffn_over"], 1)
            sp.dma_start(wf1s, wf1).then_inc(S["attn_in"], 16)
            sp.dma_start(wbs, wb).then_inc(S["attn_in"], 16)
            sp.dma_start(hw, head_w[0]).then_inc(S["head_in"], 16)
            sp.dma_start(tw, tail_w[0]).then_inc(S["tail_in"], 16)
            sp.wait_ge(S["silu_head"], 3)
            sp.dma_start(hw, head_w[1]).then_inc(S["head_in"], 16)
            sp.wait_ge(S["silu_head"], 6)
            sp.dma_start(hw, head_w[2]).then_inc(S["head_in"], 16)
            with sp.Fori(1, H - 2) as h:
                sp.wait_ge(S["wo_full"], 4 * h)
                sp.dma_start(tw, tail_w[bass.ds(h, 1)]).then_inc(S["tail_in"], 16)
                sp.wait_ge(S["silu_head"], 3 * h + 6)
                sp.dma_start(hw, head_w[bass.ds(h + 2, 1)]).then_inc(S["head_in"], 16)
            for h in range(H - 2, H):
                sp.wait_ge(S["wo_full"], 4 * h)
                sp.dma_start(tw, tail_w[h]).then_inc(S["tail_in"], 16)
            sp.wait_ge(S["attn_over"], 1)
            ffn(1)
            sp.wait_ge(S["ffn_over"], 2)
            sp.dma_start(out.rearrange("n p d -> p n d"), x_res[:, :, :]).then_inc(S["stored"], 16)
            sp.wait_ge(S["stored"], 16)

        @block.gpsimd
        def _(pool):
            nc.gpsimd.memset(ident[:, :], 0.0).then_inc(S["consts"], 1)
            nc.gpsimd.memset(ones[:, :], 1.0).then_inc(S["consts"], 1)
            nc.gpsimd.memset(masks[:, :, :], 1.0).then_inc(S["consts"], 1)
            nc.gpsimd.memset(eps_ln[:, :], 1e-5).then_inc(S["consts"], 1)
            nc.gpsimd.memset(eps_l2[:, :], 1e-6).then_inc(S["consts"], 1)
            nc.gpsimd.iota(small[0:NE, 1, 0:1].bitcast(i32), pattern=[[0, 1]], base=0,
                           channel_multiplier=1).then_inc(S["pid"], 1)
            nc.gpsimd.memset(sco[:, :, NE:NE + 2], -1.0).then_inc(S["pads_made"], 1)
            pool.wait_ge(S["consts"], 5)
            nc.gpsimd.affine_select(out=ident[:, :], in_=ident[:, :], compare_op=ALU.not_equal, fill=1.0,
                                    base=0, pattern=[[-1, P]], channel_multiplier=1).then_inc(S["consts"], 1)
            for l in range(LEVELS):
                m = 1 << l
                mk = masks[:, l, :].rearrange("p (n m) -> p n m", m=m)
                nc.gpsimd.affine_select(out=mk, in_=mk, compare_op=ALU.is_ge, fill=0.0, base=0,
                                        pattern=[[-2 * m, 64 // m], [0, m]],
                                        channel_multiplier=1).then_inc(S["consts"], 1)
                pool.wait_ge(S["consts"], 7 + 2 * l)
                nc.gpsimd.affine_select(out=mk, in_=mk, compare_op=ALU.is_ge, fill=0.0, base=m - 1,
                                        pattern=[[2 * m, 64 // m], [0, m]],
                                        channel_multiplier=-1).then_inc(S["consts"], 1)
            pool.wait_ge(S["ffn_over"], 1)
            for l in range(LEVELS):
                nc.gpsimd.memset(bt[l], 0.0).then_inc(S["zeros_pool"], 1)

            def set_w(h, g, t, fresh):
                if not fresh:
                    pool.wait_ge(S["u1_full"], t - 1)
                nc.gpsimd.tensor_tensor(
                    vw[:, :, 4 * g:4 * g + 4, :],
                    ident[:, :].unsqueeze(1).unsqueeze(1).broadcast_to([P, 2, 4, P]),
                    beta[:, bass.ds(h, 1), 4 * g:4 * g + 4].broadcast_to([P, 2, 4])
                    .unsqueeze(3).broadcast_to([P, 2, 4, P]), ALU.mult).then_inc(S["vw_set"], 1)

            def set_diagonal(h, g, t, fresh):
                pool.wait_ge(S["pj_free"], turn_base(h))
                if not fresh:
                    pool.wait_ge(S["o1_full"], t - 1)
                nc.gpsimd.tensor_tensor(
                    aq[:, 4 * g:4 * g + 4, :], ident[:, :].unsqueeze(1).broadcast_to([P, 4, P]),
                    diag[:, 4 * g:4 * g + 4].unsqueeze(2).broadcast_to([P, 4, P]), ALU.mult).then_inc(S["aq_set"], 1)

            def level(l, g, t):
                m = 1 << l
                nb = 4 * 64 // m
                pool.wait_ge(S["al_full"], 7 * t + l + 1)
                if l == 0:
                    pool.wait_ge(S["kr_set"], t + 1)
                else:
                    pool.wait_ge(S["tot_made"], 6 * t + l)
                    pool.wait_ge(S["lvl_upd"], 14 * t + 2 * l)
                n = 4 * P >> l
                t2 = tot[l][:, g * n:(g + 1) * n].rearrange("p (b s) -> p b s", s=2)
                k2 = kq[:, :, 4 * g:4 * g + 4, :].rearrange("p z u t -> p z (u t)")
                k2 = k2.rearrange("p z (b s m) -> p z b s m", s=2, m=m)[:, :, :, 1, :]
                nc.gpsimd.tensor_tensor(
                    k2, k2, t2[:, :, 0].unsqueeze(1).unsqueeze(3).broadcast_to([P, 2, nb, m]),
                    ALU.mult).then_inc(S["lvl_upd"], 1)
                r2 = kr[:, 4 * g:4 * g + 4, :].rearrange("p u t -> p (u t)")
                r2 = r2.rearrange("p (b s m) -> p b s m", s=2, m=m)[:, :, 0, :]
                nc.gpsimd.tensor_tensor(
                    r2, r2, t2[:, :, 1].unsqueeze(2).broadcast_to([P, nb, m]),
                    ALU.mult).then_inc(S["lvl_upd"], 1)
                if l < LEVELS - 1:
                    nc.gpsimd.tensor_tensor(tot[l + 1][:, g * n // 2:(g + 1) * n // 2], t2[:, :, 0],
                                            t2[:, :, 1], ALU.mult).then_inc(S["tot_made"], 1)

            def multiply(hp):
                pool.wait_ge(S["qk_made"], 2 * hp + 2)
                nc.gpsimd.tensor_tensor(prod, qk[:, 0, :], qk[:, 1, :], ALU.mult).then_inc(S["prod_made"], 1)

            def turn(h, first, prep):
                for s in range(14):
                    g, l = s // LEVELS, s % LEVELS
                    level(l, g, 2 * h + g)
                    if s == 5:
                        set_w(h, 1, 2 * h + 1, first)
                        set_diagonal(h, 1, 2 * h + 1, first)
                    if s == 11 and prep:
                        set_w(h + 1, 0, 2 * h + 2, False)
                        multiply(h + 1)
                    if s == 12 and prep:
                        set_diagonal(h + 1, 0, 2 * h + 2, False)

            pool.wait_ge(S["beta_made"], 1)
            set_w(0, 0, 0, True)
            multiply(0)
            set_diagonal(0, 0, 0, True)
            turn(0, True, True)
            with pool.Fori(1, H - 1) as h:
                turn(h, False, True)
            turn(H - 1, False, False)

        @block.scalar
        def _(act):
            act.wait_ge(S["consts"], 6 + 2 * LEVELS)

            def layernorm(k):
                act.wait_ge(S["ln_var"], k + 1)
                nc.scalar.activation(lnv[:, 1, :], lnv[:, 0, :], ACT.Ln).then_inc(S["ln_step"], 1)
                act.wait_ge(S["ln_step"], k + 1)
                nc.scalar.activation(lnv[:, 1, :], lnv[:, 1, :], ACT.Exp, scale=-0.5).then_inc(S["ln_rs"], 1)
                for j in range(4):
                    act.wait_ge(S["ln_tr"], 4 * k + j + 1)
                    nc.scalar.copy(xnT[:, :, j * 256:(j + 1) * 256],
                                   pb[j % 2][:, :].rearrange("p (k t) -> p k t", k=KT)).then_inc(S["ln_ev"], 1)

            def ffn(q):
                layernorm(2 * q)
                act.wait_ge(S["rt_shift"], q + 1)
                nc.scalar.activation(lgt[:, :, 0:NE], lgt[:, :, 0:NE], ACT.Exp).then_inc(S["rt_exp"], 1)

                def shared(hh):
                    for m in range(3):
                        mw = min(P, ISH - m * P)
                        act.wait_ge(S["sh_gate"], 6 * q + 3 * hh + m + 1)
                        nc.scalar.activation(shs[m][0:mw], pb[2 * m][0:mw, :], ACT.Silu).then_inc(S["sh_silu"], 1)

                shared(0)
                for j in range(2):
                    act.wait_ge(S["rt_wdt_tr"], 2 * q + j + 1)
                    nc.scalar.copy(wdT[:, j * 512:(j + 1) * 512], pb[j][0:NE, :]).then_inc(S["rt_wdt"], 1)
                act.wait_ge(S["rt_mshift"], q + 1)
                nc.scalar.activation(soft, soft, ACT.Exp).then_inc(S["rt_mexp"], 1)
                shared(1)
                for j in range(2):
                    act.wait_ge(S["rt_soft_tr"], 2 * q + j + 1)
                    nc.scalar.copy(softT[:, j * 512:(j + 1) * 512], pb[j][0:NE, :]).then_inc(S["rt_softT"], 1)

                def spread(g, par):
                    act.wait_ge(S["we_full"], g + 1)
                    nc.scalar.copy(wes[par], pb[2][:, :]).then_inc(S["we_ev"], 1)

                def step(g, hh, last):
                    act.wait_ge(S["gu_full"], 3 * g + 1)
                    nc.scalar.activation(sg0, pb[4][:, :], ACT.Silu).then_inc(S["silu_done"], 1)
                    act.wait_ge(S["gu_full"], 3 * g + 3)
                    nc.scalar.activation(sg2[0:64], pb[6][0:64, :], ACT.Silu).then_inc(S["silu_done"], 1)
                    if not last:
                        spread(g + 1, 1 - hh)

                spread(STEPS * q, 0)
                with act.Fori(0, F // 2 - 1) as i:
                    for j in range(4):
                        step(4 * i + (STEPS * q + j), j % 2, False)
                for j in range(4):
                    step(STEPS * (q + 1) - 4 + j, j % 2, j == 3)

            ffn(0)
            act.wait_ge(S["ffn_over"], 1)
            layernorm(1)
            act.wait_ge(S["beta_full"], 1)
            nc.scalar.activation(ebeta, pb[4][:, 0:NT * H].rearrange("p (n h) -> p n h", n=NT),
                                 ACT.Exp, scale=-1.0).then_inc(S["beta_exp"], 1)
            for hh in range(2):
                act.wait_ge(S["xf_full"], hh + 1)
                nc.scalar.copy(xfT[:, hh * HALF:(hh + 1) * HALF], pb[5 + hh][:, :]).then_inc(S["xf_ev"], 1)
            act.wait_ge(S["zeros_dve"], LEVELS + 1)

            def half(ap, hh):
                return ap[:, hh * HALF:(hh + 1) * HALF]

            def units(bank):
                return bank[:, 0:2 * P].rearrange("p (u t) -> p u t", u=2)

            def chunk(buf, g, c):
                return buf[:, 4 * g:4 * g + 4, :].rearrange("p (s c) t -> p s c t", c=2)[:, :, c, :]

            def tail(s, g, t):
                if s == 0:
                    act.wait_ge(S["u0_full"], t + 1)
                    nc.scalar.copy(chunk(uu, g, 0), units(pb[T0])).then_inc(S["u0_ev"], 1)
                    act.wait_ge(S["krt_full"], t + 1)
                    nc.scalar.copy(krt[:, 2 * g:2 * g + 2, :], units(pb[T1])).then_inc(S["krt_ev"], 1)
                if s == 1:
                    act.wait_ge(S["o0_full"], t + 1)
                    nc.scalar.copy(chunk(oT, g, 0), units(pb[T1])).then_inc(S["o0_ev"], 1)
                if s == 3:
                    act.wait_ge(S["u1_full"], t + 1)
                    nc.scalar.copy(chunk(uu, g, 1), units(pb[T1])).then_inc(S["u1_ev"], 1)
                if s == 4:
                    act.wait_ge(S["o1_full"], t + 1)
                    nc.scalar.copy(chunk(oT, g, 1), units(pb[T0])).then_inc(S["o1_ev"], 1)
                    act.wait_ge(S["o1_ev"], t + 1)
                    nc.scalar.activation(half(sqo, g), oT[:, 4 * g:4 * g + 4, :].rearrange("p u t -> p (u t)"),
                                         ACT.Square).then_inc(S["sqo_made"], 1)
                if s == 5:
                    act.wait_ge(S["n_full"], t + 1)
                    nc.scalar.activation(half(sqo, g), pb[T1][:, :], ACT.Ln, bias=eps_ln[:, :],
                                         scale=1.0 / P).then_inc(S["n_ln"], 1)
                    act.wait_ge(S["n_ln"], t + 1)
                    nc.scalar.activation(half(sqo, g), half(sqo, g), ACT.Exp, scale=-0.5).then_inc(S["rno_made"], 1)

            def turn(h, hp, first, delta, prep):
                names = TURN if delta and prep else (NEXT if prep else OWN)
                base = turn_base(h) if delta else 0

                def arrive(name):
                    act.wait_ge(S["pj_full"], base + (names.index(name) + 1))
                    return pb[5 + names.index(name) % 2]

                def evacuate(name):
                    kind, hh = name[:-1], int(name[-1])
                    if kind in ("k", "q", "v"):
                        z = ("k", "q", "v").index(kind)
                        if name == "k0":
                            act.wait_ge(S["head_in"], 16 * hp + 16)
                        seqs = arrive(name)[:, :].rearrange("p (s t) -> p s t", s=2)
                        nc.scalar.copy(raw[:, z, 2 * hh:2 * hh + 2, 3:3 + T], seqs)
                        nc.scalar.activation(acc[:, z, 2 * hh:2 * hh + 2, :], seqs, ACT.Copy,
                                             scale=hw[:, C_CONV + 4 * z + 3:C_CONV + 4 * z + 4]
                                             ).then_inc(S["pj_free"], 1)
                    elif kind == "vt":
                        if not first:
                            act.wait_ge(S["r1_made"], 2 * h + (hh - 1))
                        nc.scalar.copy(vtok[:, 4 * hh:4 * hh + 4, :],
                                       arrive(name)[:, :].rearrange("p (u t) -> p u t", u=4)).then_inc(S["pj_free"], 1)
                    elif kind == "g":
                        nc.scalar.activation(half(zg, hh), arrive(name)[:, :], ACT.Identity,
                                             bias=hw[:, C_DT:C_DT + 1]).then_inc(S["pj_free"], 1)
                    elif kind == "gt":
                        if hh == 0:
                            act.wait_ge(S["tail_in"], 16 * h + 16)
                        if not first:
                            act.wait_ge(S["wo_full"], 4 * h + 2 * (hh - 1))
                        nc.scalar.activation(gate[:, 4 * hh:4 * hh + 4, :],
                                             arrive(name)[:, :].rearrange("p (u t) -> p u t", u=4), ACT.Silu,
                                             bias=tw[:, C_BG:C_BG + 1]).then_inc(S["pj_free"], 1)
                    elif kind in ("sk", "sq"):
                        z = ("sk", "sq").index(kind)
                        nc.scalar.activation(half(rn[:, z, :], hh), arrive(name)[:, :], ACT.Ln,
                                             bias=eps_l2[:, :]).then_inc(S["pj_free"], 1)
                        if hh == 1:
                            act.wait_ge(S["pj_free"], base + (names.index(name) + 1))
                            nc.scalar.activation(rn[:, z, :], rn[:, z, :], ACT.Exp, scale=-0.5).then_inc(S["rn_made"], 1)
                    else:
                        nc.scalar.copy(diag[:, 4 * hh:4 * hh + 4], arrive(name)[:, 0:4]).then_inc(S["pj_free"], 1)

                def silu(z, target):
                    act.wait_ge(S["conv_tap"], 18 * hp + 6 * z + 6)
                    nc.scalar.activation(target, acc[:, z].rearrange("p s t -> p (s t)"),
                                         ACT.Silu).then_inc(S["silu_head"], 1)

                def square(z):
                    act.wait_ge(S["silu_head"], 3 * hp + z + 1)
                    nc.scalar.activation(acc[:, z].rearrange("p s t -> p (s t)"), kqs[:, z, :],
                                         ACT.Square).then_inc(S["sq_head"], 1)

                for s in range(14):
                    g, l = s // LEVELS, s % LEVELS
                    t = 2 * h + g if delta else None
                    if delta:
                        m = 1 << l
                        act.wait_ge(S["p_full"], 7 * t + l + 1)
                        nc.scalar.copy(
                            halves(pt[l][:, 4 * g:4 * g + 4, :].rearrange("p u t -> p (u t)"), m, 0),
                            pb[2][:, 0:256].rearrange("p (n m) -> p n m", m=m)).then_inc(S["p_ev"], 1)
                    if s == 6 and prep:
                        nc.scalar.activation(nega[:, 0:1], hw[:, C_AL:C_AL + 1], ACT.Exp).then_inc(S["ea_made"], 1)
                    if s == 9:
                        act.preload_act_table_set("natural_log_exp_and_others")
                    for name in SLOTS[s]:
                        if name in names:
                            evacuate(name)
                    if s == 6 and prep:
                        act.wait_ge(S["pj_free"], base + (names.index("g1") + 1))
                        nc.scalar.activation(eg, zg, ACT.Abs).then_inc(S["g_step"], 1)
                        act.wait_ge(S["g_step"], 3 * hp + 1)
                        nc.scalar.activation(eg, eg, ACT.Exp, scale=-1.0).then_inc(S["g_step"], 1)
                        act.wait_ge(S["g_step"], 3 * hp + 2)
                        nc.scalar.activation(eg, eg, ACT.Ln, bias=1.0).then_inc(S["g_step"], 1)
                    if s == 7:
                        act.preload_act_table_set("silu_and_others")
                    if s == 7 and prep:
                        silu(0, kqs[:, 0, :])
                        silu(1, kqs[:, 1, :])
                        square(0)
                    if s == 8 and prep:
                        square(1)
                        silu(2, vs)
                    if s == 10 and prep:
                        act.wait_ge(S["sp_made"], hp + 1)
                        act.wait_ge(S["na_made"], hp + 1)
                        if delta:
                            act.wait_ge(S["tot_made"], 12 * h + 7)
                        nc.scalar.activation(ge, zg, ACT.Exp, scale=nega[:, 1:2]).then_inc(S["ge_made"], 1)
                    if delta and not (first and g == 0):
                        tail(l, 1 - g, t - 1)

            act.preload_act_table_set("natural_log_exp_and_others")
            turn(None, 0, False, False, True)
            turn(0, 1, True, True, True)
            with act.Fori(1, H - 1) as h:
                turn(h, h + 1, False, True, True)
            turn(H - 1, None, False, True, False)
            for s in range(LEVELS):
                tail(s, 1, 2 * H - 1)
            act.wait_ge(S["attn_over"], 1)
            ffn(1)

        @block.vector
        def _(dve):
            V = nc.vector
            chain = [0]

            def link(ins):
                chain[0] += 1
                ins.then_inc(S["rt_chain"], 1)
                dve.wait_ge(S["rt_chain"], chain[0])

            inv_f, neg_f, pid_f = small[0:NE, 2, :], small[0:NE, 3, :], small[0:NE, 4, 0:1]
            dve.wait_ge(S["inv_in"], 16)
            dve.wait_ge(S["pid"], 1)
            V.tensor_copy(inv_f, small[0:NE, 0, :].bitcast(i32))
            link(V.tensor_copy(pid_f, small[0:NE, 1, 0:1].bitcast(i32)))
            link(V.tensor_scalar(neg_f, inv_f, 0.0, float(NE), ALU.is_lt, ALU.mult))
            link(V.tensor_tensor(inv_f, inv_f, neg_f, ALU.add))
            link(V.tensor_scalar(inv_f, inv_f, 0.0, float(NE - 1), ALU.max, ALU.min))
            V.tensor_scalar(onehot[:, :], inv_f, pid_f, None, ALU.is_equal).then_inc(S["onehot_made"], 1)
            dve.wait_ge(S["pads_made"], 1)

            def layernorm(k):
                for n in range(NT):
                    V.bn_stats(stats[:, n, :], x_res[:, n, :]).then_inc(S["ln_stats"], 1)
                dve.wait_ge(S["ln_stats"], NT * (k + 1))
                for n in range(NT):
                    last = V.bn_aggr(mv[:, n, :], stats[:, n, :])
                link(last)
                var, y, t = lnv[:, 0, :], lnv[:, 1, :], lnv[:, 2, :]
                V.tensor_scalar(var, mv[:, :, 1], 1e-5, None, ALU.add).then_inc(S["ln_var"], 1)
                dve.wait_ge(S["ln_rs"], k + 1)
                dve.wait_ge(S["ln_var"], k + 1)
                link(V.tensor_tensor(t, var, y, ALU.mult))
                link(V.tensor_tensor(t, t, y, ALU.mult))
                link(V.tensor_scalar(t, t, -0.5, 1.5, ALU.mult, ALU.add))
                link(V.tensor_tensor(lnv[:, 3, :], y, t, ALU.mult))
                for n in range(NT):
                    V.tensor_scalar(xn[:, n, :], x_res[:, n, :], mv[:, n, 0:1], lnv[:, 3, n:n + 1],
                                    ALU.subtract, ALU.mult).then_inc(S["ln_xn"], 1)

            def ffn(q):
                layernorm(2 * q)
                if q == 1:
                    link(V.memset(sco[:, :, NE:NE + 2], -1.0))
                mx, sm = small[:, 0, 0:NT], small[:, 1, 0:NT]
                dve.wait_ge(S["rt_logits"], q + 1)
                lg = pb[7][:, :].rearrange("p (n e) -> p n e", n=NT)
                link(V.reduce_max(mx, lg, AX.X))
                V.tensor_tensor(lgt[:, :, 0:NE], lg, mx.unsqueeze(2).broadcast_to([P, NT, NE]),
                                ALU.subtract).then_inc(S["rt_shift"], 1)
                dve.wait_ge(S["rt_exp"], q + 1)
                link(V.reduce_sum(sm, lgt[:, :, 0:NE], AX.X))
                link(V.reciprocal(sm, sm))
                link(V.tensor_tensor(sco[:, :, 0:NE], lgt[:, :, 0:NE],
                                     sm.unsqueeze(2).broadcast_to([P, NT, NE]), ALU.mult))
                for n in range(NT):
                    last = V.max(top8[:, n, :], sco[:, n, 0:NE])
                link(last)
                link(V.memset(top8[:, :, TOPK:8], -1.0))
                for n in range(NT):
                    last = V.match_replace(lgt[:, n, :], top8[:, n, :], sco[:, n, :], 0.0)
                link(last)
                V.tensor_tensor(wd, sco[:, :, 0:NE], lgt[:, :, 0:NE], ALU.subtract).then_inc(S["rt_wd"], 1)

                def shared(hh):
                    for m in range(3):
                        mw = min(P, ISH - m * P)
                        dve.wait_ge(S["sh_silu"], 6 * q + 3 * hh + m + 1)
                        dve.wait_ge(S["sh_up"], 6 * q + 3 * hh + m + 1)
                        V.tensor_tensor(shh[m][0:mw], shs[m][0:mw], pb[2 * m + 1][0:mw, :],
                                        ALU.mult).then_inc(S["sh_h"], 1)
                    for j in range(2):
                        dve.wait_ge(S["sh_out"], 4 * q + 2 * hh + j + 1)
                        xv = x_res[:, 4 * hh + 2 * j:4 * hh + 2 * j + 2, :].rearrange("p n d -> p (n d)")
                        V.scalar_tensor_tensor(out=xv, in0=pb[6 + j][:, :], scalar=0.5, in1=xv,
                                               op0=ALU.mult, op1=ALU.add).then_inc(S["out_acc"], 1)

                shared(0)
                dve.wait_ge(S["rt_flat"], q + 1)
                link(V.tensor_copy(flat, pb[2][:, :].rearrange("p (a k) -> p a k", k=K8)))
                sums, mk = small[:, 2, :], small[:, 3, :]
                link(V.reduce_sum(sums, flat, AX.X))
                V.tensor_scalar(half_scal.rearrange("p (f n) -> p n f", f=F),
                                sums.rearrange("p (n f) -> p n f", n=NT), 0.5, None, ALU.mult)
                link(V.tensor_scalar(soft, flat, 0.0, -1e9, ALU.is_equal, ALU.mult))
                link(V.tensor_tensor(soft, soft, flat, ALU.add))
                link(V.reduce_max(mk, soft, AX.X))
                V.tensor_tensor(soft, soft, mk.unsqueeze(2).broadcast_to([P, NT * F, K8]),
                                ALU.subtract).then_inc(S["rt_mshift"], 1)
                dve.wait_ge(S["rt_mexp"], q + 1)
                link(V.reduce_sum(mk, soft, AX.X))
                link(V.reciprocal(mk, mk))
                V.tensor_tensor(soft, soft, mk.unsqueeze(2).broadcast_to([P, NT * F, K8]),
                                ALU.mult).then_inc(S["rt_soft"], 1)

                def scale_weights(gf, i, pf):
                    dve.wait_ge(EW_IN[pf], 48 * i + 48 * (4 * q + 1))
                    V.tensor_tensor(ew[pf][:, C_QB:C_D1], ew[pf][:, C_QB:C_D1], es[pf][:, 0:384], ALU.mult)
                    V.tensor_tensor(ew[pf][64:P, C_D2:C_DQ], ew[pf][64:P, C_D2:C_DQ],
                                    es[pf][64:P, 384:640], ALU.mult).then_inc(S["scaled"], 1)

                def add_w(g, par):
                    dve.wait_ge(S["x_full"], g + 1)
                    for kt in range(KT):
                        last = V.tensor_tensor(xe[par][:, kt, :], pb[kt][:, :],
                                               xnT[:, kt, par * HALF:(par + 1) * HALF], ALU.add)
                    last.then_inc(S["xe_made"], 1)

                def weigh(g, par):
                    dve.wait_ge(S["a_made"], g + 1)
                    dve.wait_ge(S["we_ev"], g + 1)
                    V.tensor_tensor(aw, pb[3][:, :], wes[par], ALU.mult).then_inc(S["aw_made"], 1)

                def step(g, i, pf, hh, last):
                    dve.wait_ge(S["silu_done"], 2 * g + 1)
                    dve.wait_ge(S["gu_full"], 3 * g + 2)
                    V.tensor_tensor(h1[hh], sg0, pb[5][:, :], ALU.mult).then_inc(S["h_made"], 1)
                    dve.wait_ge(S["silu_done"], 2 * g + 2)
                    V.tensor_tensor(h2[hh][0:64], sg2[0:64], pb[6][64:P, :], ALU.mult).then_inc(S["h_made"], 1)
                    if not last:
                        add_w(g + 1, 1 - hh)
                        if hh == 1:
                            scale_weights(None, i + pf, 1 - pf)
                    dve.wait_ge(S["da_full"], g + 1)
                    V.tensor_tensor(h2[hh][64:P], pb[7][64:P, :], wes[hh][64:P], ALU.mult).then_inc(S["daw_made"], 1)
                    if not last:
                        weigh(g + 1, 1 - hh)
                    for j in range(2):
                        dve.wait_ge(S["out_full"], 2 * g + j + 1)
                        for t in range(2):
                            n = 4 * hh + 2 * j + t
                            acc_op = V.scalar_tensor_tensor(
                                out=x_res[:, n, :], in0=pb[5 + j][:, t * D:(t + 1) * D],
                                scalar=half_scal[:, bass.ds(2 * NT * i + (pf * NT + n), 1)]
                                if not isinstance(i, int) else
                                half_scal[:, 2 * NT * i + pf * NT + n:2 * NT * i + pf * NT + n + 1],
                                in1=x_res[:, n, :], op0=ALU.mult, op1=ALU.add)
                        acc_op.then_inc(S["out_acc"], 1)

                scale_weights(8 * q, 0, 0)
                shared(1)
                add_w(STEPS * q, 0)
                weigh(STEPS * q, 0)
                with dve.Fori(0, F // 2 - 1) as i:
                    for j in range(4):
                        step(4 * i + (STEPS * q + j), i, j // 2, j % 2, False)
                for j in range(4):
                    step(STEPS * (q + 1) - 4 + j, F // 2 - 1, j // 2, j % 2, j == 3)
                dve.wait_ge(S["out_acc"], ACCS * (q + 1))
                V.tensor_copy(lnv[:, 2, 0:1], x_res[:, 0, 0:1]).then_inc(S["ffn_over"], 1)

            dve.wait_ge(S["x_in"], 32)
            ffn(0)
            dve.wait_ge(S["ffn_over"], 1)
            for l in range(LEVELS):
                V.memset(pt[l], 0.0).then_inc(S["zeros_dve"], 1)
            V.memset(raw[:, :, :, 0:3].rearrange("p z s t -> p (z s) t"), 0.0).then_inc(S["zeros_dve"], 1)
            layernorm(1)
            dve.wait_ge(S["beta_exp"], 1)
            link(V.tensor_scalar(ebeta, ebeta, 1.0, None, ALU.add))
            V.reciprocal(beta, ebeta.rearrange("p n h -> p h n")).then_inc(S["beta_made"], 1)
            dve.wait_ge(S["zeros_pool"], LEVELS)

            def set_up(h, g, t, fresh):
                cols = slice(g * HALF, (g + 1) * HALF)
                dve.wait_ge(S["qk_made"], 2 * h + 2)
                dve.wait_ge(S["ge_made"], h + 1)
                if not fresh:
                    dve.wait_ge(S["o1_full"], t - 1)
                V.tensor_tensor(kq[:, :, 4 * g:4 * g + 4, :].rearrange("p z u t -> p z (u t)"), qk[:, :, cols],
                                ge[:, cols].unsqueeze(1).broadcast_to([P, 2, HALF]), ALU.mult)
                V.tensor_copy(kr[:, 4 * g:4 * g + 4, :].rearrange("p u t -> p (u t)"),
                              qk[:, 0, cols]).then_inc(S["kr_set"], 1)

            def mask(l, g, t):
                m = 1 << l
                mk = masks[:, l, :].rearrange("p (n m) -> p n m", m=m).unsqueeze(1).broadcast_to([P, 4, 64 // m, m])
                bank = pb[(l + g) % 2][:, :].rearrange("p (u z n m) -> p u z n m", u=4, z=2, m=m)

                def second(buf):
                    return buf[:, 4 * g:4 * g + 4, :].rearrange("p u (n s m) -> p u n s m", s=2, m=m)[:, :, :, 1, :]

                if l == 0:
                    dve.wait_ge(S["aq_set"], t + 1)
                else:
                    dve.wait_ge(S["masked"], 14 * t + 2 * l)
                dve.wait_ge(S["al_full"], 7 * t + l + 1)
                V.tensor_tensor(second(bt[l]), bank[:, :, 0], mk, ALU.mult).then_inc(S["masked"], 1)
                V.copy_predicated(second(aq), mk.bitcast(u32), bank[:, :, 1]).then_inc(S["masked"], 1)

            def grow(l, g, t):
                m = 1 << l
                dve.wait_ge(S["d_full"], 7 * t + l + 1)
                if l == 0:
                    dve.wait_ge(S["vw_set"], t + 1)
                for z in range(2 if l < LEVELS - 1 else 1):
                    part = vw[:, z, 4 * g:4 * g + 4, :].rearrange("p u (n s m) -> p (u n) s m", s=2, m=m)[:, :, 1 - z, :]
                    V.tensor_tensor(part, part, pb[3][:, z * 256:(z + 1) * 256].rearrange("p (n m) -> p n m", m=m),
                                    ALU.subtract).then_inc(S["vw_upd"], 1)

            def tail(s, g, t):
                def two(bank):
                    return bank[:, 0:2 * P].rearrange("p (u t) -> p u t", u=2)

                if s == 1:
                    dve.wait_ge(S["s_full"], t + 1)
                    V.tensor_copy(state[:, 2 * g:2 * g + 2, :], two(pb[T0])).then_inc(S["s_ev"], 1)
                if s == 2:
                    dve.wait_ge(S["ks_full"], t + 1)
                    V.tensor_tensor(r1[:, 2 * g:2 * g + 2, :],
                                    vtok[:, 4 * g:4 * g + 4, :].rearrange("p (s c) t -> p s c t", c=2)[:, :, 1, :],
                                    two(pb[T0]), ALU.subtract).then_inc(S["r1_made"], 1)
                gf = gate[:, 4 * g:4 * g + 4, :].rearrange("p u t -> p (u t)")
                if s == 4:
                    dve.wait_ge(S["o1_ev"], t + 1)
                    V.scalar_tensor_tensor(out=gf, in0=oT[:, 4 * g:4 * g + 4, :].rearrange("p u t -> p (u t)"),
                                           scalar=tw[:, C_ON:C_ON + 1], in1=gf,
                                           op0=ALU.mult, op1=ALU.mult).then_inc(S["gm_made"], 1)
                if s == 5:
                    dve.wait_ge(S["rno_made"], t + 1)
                    dve.wait_ge(S["gm_made"], t + 1)
                    V.tensor_tensor(gf, gf, sqo[:, g * HALF:(g + 1) * HALF], ALU.mult).then_inc(S["on_made"], 1)
                if s == 6:
                    for j in range(2):
                        dve.wait_ge(S["wo_full"], 2 * t + j + 1)
                        xv = x_res[:, 4 * g + 2 * j:4 * g + 2 * j + 2, :].rearrange("p n d -> p (n d)")
                        V.tensor_tensor(xv, xv, pb[(T0, T1)[j]][:, :], ALU.add).then_inc(S["wo_acc"], 1)

            def turn(h, hp, first, delta, prep):
                names = TURN if delta and prep else (NEXT if prep else OWN)
                base = turn_base(h) if delta else 0

                def conv(name):
                    z, hh = ("k", "q", "v").index(name[0]), int(name[1])
                    seqs = slice(2 * hh, 2 * hh + 2)
                    dve.wait_ge(S["pj_free"], base + (names.index(name) + 1))
                    for n, i in enumerate((2, 1, 0)):
                        if n:
                            dve.wait_ge(S["conv_tap"], 18 * hp + 6 * z + 3 * hh + n)
                        V.scalar_tensor_tensor(out=acc[:, z, seqs], in0=raw[:, z, seqs, i:i + T],
                                               scalar=hw[:, C_CONV + 4 * z + i:C_CONV + 4 * z + i + 1],
                                               in1=acc[:, z, seqs], op0=ALU.mult, op1=ALU.add).then_inc(S["conv_tap"], 1)

                for s in range(14):
                    g, l = s // LEVELS, s % LEVELS
                    if delta:
                        t = 2 * h + g
                        if l < LEVELS - 1:
                            mask(l + 1, g, t)
                        elif g == 0:
                            mask(0, 1, t + 1)
                        elif prep:
                            mask(0, 0, t + 1)
                        grow(l, g, t)
                        if not (first and g == 0):
                            tail(l, 1 - g, t - 1)
                        if s == 4:
                            set_up(h, 1, 2 * h + 1, first)
                    if not prep:
                        continue
                    for name in {1: ["k0"], 2: ["k1", "q0"], 3: ["q1"], 5: ["v0"], 6: ["v1"]}.get(s, []):
                        conv(name)
                    if s == 7:
                        dve.wait_ge(S["ea_made"], hp + 1)
                        V.tensor_scalar(nega[:, 1:2], nega[:, 0:1], -1.0, None, ALU.mult).then_inc(S["na_made"], 1)
                        dve.wait_ge(S["g_step"], 3 * hp + 3)
                        V.scalar_tensor_tensor(out=zg, in0=zg, scalar=0.0, in1=eg, op0=ALU.max,
                                               op1=ALU.add).then_inc(S["sp_made"], 1)
                    if s == 9:
                        dve.wait_ge(S["rn_made"], 2 * hp + 1)
                        V.tensor_tensor(qk[:, 0, :], kqs[:, 0, :], rn[:, 0, :], ALU.mult).then_inc(S["qk_made"], 1)
                    if s == 10:
                        dve.wait_ge(S["rn_made"], 2 * hp + 2)
                        V.scalar_tensor_tensor(out=qk[:, 1, :], in0=kqs[:, 1, :], scalar=float(P) ** -0.5,
                                               in1=rn[:, 1, :], op0=ALU.mult, op1=ALU.mult).then_inc(S["qk_made"], 1)
                    if s == 11:
                        if delta:
                            set_up(hp, 0, 2 * hp, False)
                        else:
                            set_up(0, 0, 0, True)

            turn(None, 0, False, False, True)
            mask(0, 0, 0)
            turn(0, 1, True, True, True)
            with dve.Fori(1, H - 1) as h:
                turn(h, h + 1, False, True, True)
            turn(H - 1, None, False, True, False)
            for s in range(LEVELS):
                tail(s, 1, 2 * H - 1)
            dve.wait_ge(S["wo_acc"], 4 * H)
            V.tensor_copy(lnv[:, 2, 0:1], x_res[:, 0, 0:1]).then_inc(S["attn_over"], 1)
            dve.wait_ge(S["attn_over"], 1)
            ffn(1)

        @block.tensor
        def _(pe):
            MM = nc.tensor.matmul
            pe.wait_ge(S["consts"], 6 + 2 * LEVELS)
            pe.wait_ge(S["consts_in"], 16)
            pe.wait_ge(S["onehot_made"], 1)

            def layernorm(k):
                for j in range(4):
                    pe.wait_ge(S["ln_xn"], NT * k + 2 * j + 2)
                    if j >= 2:
                        pe.wait_ge(S["ln_ev"], 4 * k + j - 1)
                    for n in range(2):
                        for kt in range(KT):
                            c = kt * 256 + n * P
                            last = nc.tensor.transpose(pb[j % 2][:, c:c + P],
                                                       xn[:, 2 * j + n, kt * P:(kt + 1) * P], ident[:, :])
                    last.then_inc(S["ln_tr"], 1)
                pe.wait_ge(S["ln_ev"], 4 * k + 4)

            def ffn(q):
                layernorm(2 * q)
                for n in range(NT):
                    for kt in range(KT):
                        last = MM(pb[7][:, n * NE:(n + 1) * NE], xnT[:, kt, n * P:(n + 1) * P],
                                  gwT[:, kt, :], start=kt == 0, stop=kt == KT - 1)
                last.then_inc(S["rt_logits"], 1)

                def shared(hh):
                    cols = slice(hh * HALF, (hh + 1) * HALF)
                    for m in range(3):
                        mw = min(P, ISH - m * P)
                        for u in range(2):
                            for kt in range(KT):
                                c = u * ISH + m * P
                                last = MM(pb[2 * m + u][0:mw, :], shw[:, kt, c:c + mw], xnT[:, kt, cols],
                                          start=kt == 0, stop=kt == KT - 1)
                            last.then_inc(S["sh_up" if u else "sh_gate"], 1)
                    pe.wait_ge(S["sh_h"], 6 * q + 3 * hh + 3)
                    for j in range(2):
                        if j == 1:
                            pe.wait_ge(S["rt_shift"], q + 1)
                        if hh:
                            pe.wait_ge(S["out_acc"], ACCS * q + j + 1)
                        for t in range(2):
                            for m in range(3):
                                mw = min(P, ISH - m * P)
                                c = (2 * j + t) * P
                                last = MM(pb[6 + j][:, t * D:(t + 1) * D], shh[m][0:mw, c:c + P],
                                          shd[0:mw, m, :], start=m == 0, stop=m == 2)
                        last.then_inc(S["sh_out"], 1)

                def turned(src, ready, made):
                    pe.wait_ge(ready, q + 1)
                    for j in range(2):
                        for t in range(4):
                            last = nc.tensor.transpose(pb[j][0:NE, t * P:(t + 1) * P], src[:, 4 * j + t, :],
                                                       ident[:, :])
                        last.then_inc(made, 1)

                pe.wait_ge(S["shared_in"], 32 * (q + 1))
                shared(0)
                turned(wd, S["rt_wd"], S["rt_wdt_tr"])
                pe.wait_ge(S["rt_wdt"], 2 * q + 2)
                for n in range(NT):
                    last = MM(pb[2][:, n * NE:(n + 1) * NE], wdT[:, n * P:(n + 1) * P], onehot[:, :],
                              start=True, stop=True)
                last.then_inc(S["rt_flat"], 1)
                pe.wait_ge(S["rt_mshift"], q + 1)
                shared(1)
                turned(soft.rearrange("p (n f) k -> p n (f k)", n=NT), S["rt_soft"], S["rt_soft_tr"])
                pe.wait_ge(S["rt_softT"], 2 * q + 2)

                def front(g, i, pf, par, first):
                    cols = slice(par * HALF, (par + 1) * HALF)
                    pe.wait_ge(EW_IN[pf], 48 * i + 48 * (4 * q + 1))
                    if not first:
                        pe.wait_ge(S["xe_made"], g)
                        pe.wait_ge(S["we_ev"], g)
                    for kt in range(KT):
                        last = MM(pb[kt][:, :], rw[pf][:, kt * P:(kt + 1) * P], softT[:, cols],
                                  start=True, stop=True)
                    last.then_inc(S["x_full"], 1)
                    MM(pb[2][:, :], rw[pf][:, 256:384], softT[:, cols],
                       start=True, stop=True).then_inc(S["we_full"], 1)

                def low_rank(g, pf, par, first):
                    pe.wait_ge(S["xe_made"], g + 1)
                    if not first:
                        pe.wait_ge(S["aw_made"], g)
                    for kt in range(KT):
                        last = MM(pb[3][:, :], ew[pf][:, C_QA + kt * P:C_QA + (kt + 1) * P], xe[par][:, kt, :],
                                  start=kt == 0, stop=kt == KT - 1)
                    last.then_inc(S["a_made"], 1)

                def step(g, gf, i, pf, hh, first, last_step):
                    for t in range(3):
                        if t == 1 and not first:
                            pe.wait_ge(S["out_acc"], 2 * g + 4 * (q + 1) - 1)
                        if t == 2 or (t == 1 and first):
                            pe.wait_ge(S["out_acc"], 2 * g + 4 * (q + 1))
                        for kt in range(KT):
                            c = C_GU + kt * 384 + t * P
                            MM(pb[4 + t][:, :], ew[pf][:, c:c + P], xe[hh][:, kt, :], start=kt == 0, stop=False)
                    pe.wait_ge(S["aw_made"], g + 1)
                    pe.wait_ge(S["scaled"], gf + 1)
                    for t in range(3):
                        MM(pb[4 + t][:, :], ew[pf][:, C_QB + t * P:C_QB + (t + 1) * P], aw,
                           start=False, stop=True).then_inc(S["gu_full"], 1)
                    if not last_step:
                        front(g + 1, i + pf if hh else i, 1 - pf if hh else pf, 1 - hh, False)
                    pe.wait_ge(S["h_made"], 2 * g + 2)
                    MM(pb[7][:, :], ew[pf][:, C_DQ:C_DQ + P], h1[hh], start=True, stop=False)
                    MM(pb[7][:, :], ew[pf][0:IR, C_DQ + P:C_DQ + 2 * P], h2[hh][0:IR], start=False,
                       stop=True).then_inc(S["da_full"], 1)
                    if not last_step:
                        low_rank(g + 1, 1 - pf if hh else pf, 1 - hh, False)
                    pe.wait_ge(S["daw_made"], g + 1)
                    for j in range(2):
                        for t in range(2):
                            c = (2 * j + t) * P
                            MM(pb[5 + j][:, t * D:(t + 1) * D], h1[hh][:, c:c + P], ew[pf][:, C_D1:C_D2],
                               start=True, stop=False)
                            last = MM(pb[5 + j][:, t * D:(t + 1) * D], h2[hh][:, c:c + P],
                                      ew[pf][:, C_D2:C_DQ], start=False, stop=True)
                        last.then_inc(S["out_full"], 1)

                front(STEPS * q, 0, 0, 0, True)
                low_rank(STEPS * q, 0, 0, True)
                with pe.Fori(0, F // 2 - 1) as i:
                    for j in range(4):
                        step(4 * i + (STEPS * q + j), 2 * i + (F * q + j // 2), i, j // 2, j % 2, j == 0, False)
                for j in range(4):
                    step(STEPS * (q + 1) - 4 + j, F * (q + 1) - 2 + j // 2, F // 2 - 1, j // 2, j % 2, False, j == 3)

            ffn(0)
            pe.wait_ge(S["ffn_over"], 1)
            layernorm(1)
            pe.wait_ge(S["attn_in"], 32)
            for n in range(NT):
                for kt in range(KT):
                    last = MM(pb[4][:, n * H:(n + 1) * H], xnT[:, kt, n * P:(n + 1) * P], wbs[:, kt, :],
                              start=kt == 0, stop=kt == KT - 1)
            last.then_inc(S["beta_full"], 1)
            for hh in range(2):
                for kt in range(KT):
                    last = MM(pb[5 + hh][:, :], wf1s[:, kt, :], xnT[:, kt, hh * HALF:(hh + 1) * HALF],
                              start=kt == 0, stop=kt == KT - 1)
                last.then_inc(S["xf_full"], 1)
            pe.wait_ge(S["xf_ev"], 2)
            pe.wait_ge(S["beta_made"], 1)

            def decayed(l, g, t, fresh):
                m = 1 << l
                if l == 0:
                    pe.wait_ge(S["kr_set"], t + 1)
                else:
                    pe.wait_ge(S["lvl_upd"], 14 * t + 2 * l)
                if not (fresh and l < 2):
                    pe.wait_ge(S["masked"], 14 * t + (2 * l - 2))
                for u in range(4):
                    rhs = kq[:, :, 4 * g + u, :].rearrange("p z (n s m) -> p z n s m", s=2, m=m)[:, :, :, 1, :]
                    last = MM(pb[(l + g) % 2][:, u * P:(u + 1) * P].rearrange("p (z n m) -> p z n m", z=2, m=m),
                              kr[:, 4 * g + u, :], rhs, start=True, stop=True)
                last.then_inc(S["al_full"], 1)

            def product(l, g, t, fresh):
                m = 1 << l
                pe.wait_ge(S["masked"], 14 * t + 2 * l + 1)
                if l == 0:
                    pe.wait_ge(S["vw_set"], t + 1)
                if not (fresh and l == 0):
                    pe.wait_ge(S["vw_upd"], 13 * t + 2 * l)
                    pe.wait_ge(S["p_ev"], 7 * t + l)
                for u in range(4):
                    last = MM(pb[2][:, u * 64:(u + 1) * 64].rearrange("p (n m) -> p n m", m=m),
                              bt[l][:, 4 * g + u, :], halves(vw[:, 1, 4 * g + u, :], m, 0), start=True, stop=True)
                last.then_inc(S["p_full"], 1)

            def growth(l, g, t):
                m = 1 << l
                pe.wait_ge(S["p_ev"], 7 * t + l + 1)
                for u in range(4):
                    n = 4 * g + u
                    last = MM(pb[3][:, u * 64:(u + 1) * 64].rearrange("p (n m) -> p n m", m=m),
                              pt[l][:, n, :], halves(vw[:, 0, n, :], m, 1), start=True, stop=True)
                    if l < LEVELS - 1:
                        last = MM(pb[3][:, 256 + u * 64:256 + (u + 1) * 64].rearrange("p (n m) -> p n m", m=m),
                                  vw[:, 0, n, :], halves(pt[l][:, n, :], m, 0), start=True, stop=True)
                last.then_inc(S["d_full"], 1)

            def tail(s, g, t, vt_done, fresh):
                def cols(bank, b):
                    return bank[:, b * P:(b + 1) * P]

                pair = ((0, 4 * g), (1, 4 * g + 2))
                if s == 0:
                    pe.wait_ge(S["vw_upd"], 13 * t + 13)
                    pe.wait_ge(S["pj_free"], vt_done)
                    if not fresh:
                        pe.wait_ge(S["wo_acc"], 2 * t)
                    for b, n in pair:
                        last = MM(cols(pb[T0], b), vw[:, 0, n, :], vtok[:, n, :], start=True, stop=True)
                    last.then_inc(S["u0_full"], 1)
                    pe.wait_ge(S["lvl_upd"], 14 * t + 14)
                    for b, n in pair:
                        last = nc.tensor.transpose(cols(pb[T1], b), kr[:, n, :], ident[:, :])
                    last.then_inc(S["krt_full"], 1)
                if s == 1:
                    pe.wait_ge(S["u0_ev"], t + 1)
                    pe.wait_ge(S["krt_ev"], t + 1)
                    for b, n in pair:
                        last = MM(cols(pb[T0], b), krt[:, 2 * g + b, :], uu[:, n, :], start=True, stop=True)
                    last.then_inc(S["s_full"], 1)
                    pe.wait_ge(S["masked"], 14 * t + 14)
                    for b, n in pair:
                        last = MM(cols(pb[T1], b), uu[:, n, :], aq[:, n, :], start=True, stop=True)
                    last.then_inc(S["o0_full"], 1)
                if s == 2:
                    pe.wait_ge(S["s_ev"], t + 1)
                    for b, n in pair:
                        last = MM(cols(pb[T0], b), kq[:, 0, n + 1, :], state[:, 2 * g + b, :], start=True, stop=True)
                    last.then_inc(S["ks_full"], 1)
                if s == 3:
                    pe.wait_ge(S["r1_made"], t + 1)
                    pe.wait_ge(S["o0_ev"], t + 1)
                    for b, n in pair:
                        last = MM(cols(pb[T1], b), vw[:, 0, n + 1, :], r1[:, 2 * g + b, :], start=True, stop=True)
                    last.then_inc(S["u1_full"], 1)
                if s == 4:
                    pe.wait_ge(S["u1_ev"], t + 1)
                    for b, n in pair:
                        MM(cols(pb[T0], b), state[:, 2 * g + b, :], kq[:, 1, n + 1, :], start=True, stop=False)
                        last = MM(cols(pb[T0], b), uu[:, n + 1, :], aq[:, n + 1, :], start=False, stop=True)
                    last.then_inc(S["o1_full"], 1)
                if s == 5:
                    pe.wait_ge(S["sqo_made"], t + 1)
                    MM(pb[T1][:, :], ones[:, :], sqo[:, g * HALF:(g + 1) * HALF], start=True,
                       stop=True).then_inc(S["n_full"], 1)
                if s == 6:
                    pe.wait_ge(S["on_made"], t + 1)
                    for j in range(2):
                        for i in range(2):
                            last = MM(pb[(T0, T1)[j]][:, i * D:(i + 1) * D], gate[:, 4 * g + 2 * j + i, :],
                                      tw[:, C_WO:C_WO + D], start=True, stop=True)
                        last.then_inc(S["wo_full"], 1)

            def turn(h, hp, first, delta, prep):
                names = TURN if delta and prep else (NEXT if prep else OWN)
                base = turn_base(h) if delta else 0

                def item(name):
                    n = names.index(name)
                    kind, hh = name[:-1], int(name[-1])
                    cols = slice(hh * HALF, (hh + 1) * HALF)
                    bank = pb[5 + n % 2]
                    if delta or n >= 2:
                        pe.wait_ge(S["pj_free"], base + (n - 1))
                    if kind in ("k", "q", "v"):
                        z = ("k", "q", "v").index(kind)
                        if name == "k0":
                            pe.wait_ge(S["head_in"], 16 * hp + 16)
                        for kt in range(KT):
                            c = C_KQV + kt * 384 + z * P
                            last = MM(bank[:, :], hw[:, c:c + P], xnT[:, kt, cols], start=kt == 0, stop=kt == KT - 1)
                    elif kind == "g":
                        last = MM(bank[:, :], hw[:, C_F2:C_F2 + P], xfT[:, cols], start=True, stop=True)
                    elif kind == "gt":
                        pe.wait_ge(S["tail_in"], 16 * h + 16)
                        for kt in range(KT):
                            last = MM(bank[:, :], tw[:, C_G + kt * P:C_G + (kt + 1) * P], xnT[:, kt, cols],
                                      start=kt == 0, stop=kt == KT - 1)
                    elif kind == "vt":
                        pe.wait_ge(S["silu_head"], 3 * h + 3)
                        for u in range(4):
                            c = (4 * hh + u) * P
                            last = nc.tensor.transpose(bank[:, u * P:(u + 1) * P], vs[:, c:c + P], ident[:, :])
                    elif kind in ("sk", "sq"):
                        z = ("sk", "sq").index(kind)
                        pe.wait_ge(S["sq_head"], 2 * hp + z + 1)
                        last = MM(bank[:, :], ones[:, :], acc[:, z].rearrange("p s t -> p (s t)")[:, cols],
                                  start=True, stop=True)
                    else:
                        pe.wait_ge(S["prod_made"], hp + 1)
                        for u in range(4):
                            c = (4 * hh + u) * P
                            last = MM(bank[:, u:u + 1], prod[:, c:c + P], ones[:, 0:1], start=True, stop=True)
                    last.then_inc(S["pj_full"], 1)

                for s in range(14):
                    g, l = s // LEVELS, s % LEVELS
                    if delta:
                        t = 2 * h + g
                        product(l, g, t, first and g == 0)
                        if l < LEVELS - 1:
                            decayed(l + 1, g, t, first and g == 0)
                        elif g == 0:
                            decayed(0, 1, t + 1, False)
                        elif prep:
                            decayed(0, 0, t + 1, False)
                    for name in SLOTS[s]:
                        if name in names:
                            item(name)
                    if delta:
                        growth(l, g, t)
                        if g == 1:
                            tail(l, 0, t - 1, own("vt0", h, not prep), first)
                        elif not first:
                            tail(l, 1, t - 1, own("vt1", h - 1, False), False)

            turn(None, 0, False, False, True)
            decayed(0, 0, 0, True)
            turn(0, 1, True, True, True)
            with pe.Fori(1, H - 1) as h:
                turn(h, h + 1, False, True, True)
            turn(H - 1, None, False, True, False)
            for s in range(LEVELS):
                tail(s, 1, 2 * H - 1, own("vt1", H - 1, True), False)
            pe.wait_ge(S["attn_over"], 1)
            ffn(1)


def kernel(**inputs):
    import numpy as np
    import concourse.bacc as bacc
    from concourse.bass_utils import run_bass_kernel_spmd

    a = {n: np.asarray(v) for n, v in inputs.items()}
    f = {n[len("L0_ffn_"):]: v for n, v in a.items() if n.startswith("L0_ffn_")}
    t = {n[len("L0_attn_"):]: v for n, v in a.items() if n.startswith("L0_attn_")}

    def tiles(w):
        return w.reshape(-1, P, w.shape[1]).transpose(1, 0, 2)

    ew = np.zeros((F, P, C_EW), np.float32)
    es = np.zeros((F, 640), np.float32)
    rw = np.zeros((F, NE, 384), np.float32)
    for g in range(F):
        gu = np.zeros((P, KT, 384), np.float32)
        for c, n in ((0, "gate_W"), (1, "up_W")):
            w = tiles(f[n][g].T)
            gu[:, :, c * P:(c + 1) * P] = w[:, :, 0:P]
            gu[:, :, 256 + 64 * c:256 + 64 * c + IR] = w[:, :, P:I]
        ew[g, :, C_GU:C_QA] = gu.reshape(P, 768)
        qa = np.zeros((P, KT, P), np.float32)
        for c, n in ((0, "gate"), (1, "up")):
            qa[:, :, 64 * c:64 * c + 64] = tiles(f[n + "_qa"][g].reshape(KR, D).T)
            qb = f[n + "_qb"][g].transpose(0, 2, 1).reshape(KR, I)
            rows = slice(64 * c, 64 * c + 64)
            ew[g, rows, C_QB + c * P:C_QB + (c + 1) * P] = qb[:, 0:P]
            ew[g, rows, C_QB + 256 + 64 * c:C_QB + 256 + 64 * c + IR] = qb[:, P:I]
            es[g, c * P:(c + 1) * P] = f[n + "_scale"][g, 0:P]
            es[g, 256 + 64 * c:256 + 64 * c + IR] = f[n + "_scale"][g, P:I]
        ew[g, :, C_QA:C_QB] = qa.reshape(P, 256)
        down = f["down_W"][g].T
        ew[g, :, C_D1:C_D2] = down[0:P]
        ew[g, 0:IR, C_D2:C_DQ] = down[P:I]
        ew[g, 64:P, C_D2:C_DQ] = f["down_qb"][g].transpose(0, 2, 1).reshape(KR, D)
        dq = f["down_qa"][g].reshape(KR, I).T
        ew[g, :, C_DQ + 64:C_DQ + P] = dq[0:P]
        ew[g, 0:IR, C_DQ + P + 64:C_DQ + 2 * P] = dq[P:I]
        es[g, 384:640] = f["down_scale"][g]
        rw[g, g * K8:(g + 1) * K8, 0:D] = f["mask_up_W"][g].T
        for c in range(2):
            for k in range(K8):
                rw[g, g * K8 + k, 256 + 64 * c + k * R:256 + 64 * c + (k + 1) * R] = 1.0
    sgu = np.ascontiguousarray(tiles(np.concatenate([f["sh_gate_W"].T, f["sh_up_W"].T], 1)))
    sdn = np.zeros((3 * P, D), np.float32)
    sdn[0:ISH] = f["sh_down_W"].T
    sdn = np.ascontiguousarray(tiles(sdn))

    hw = np.zeros((H, P, C_HW), np.float32)
    tw = np.zeros((H, P, C_TW), np.float32)
    for h in range(H):
        cols = slice(h * P, (h + 1) * P)
        for z, n in enumerate("kqv"):
            w = tiles(t["W" + n][:, cols])
            for kt in range(KT):
                hw[h, :, kt * 384 + z * P:kt * 384 + (z + 1) * P] = w[:, kt]
            hw[h, :, C_CONV + 4 * z:C_CONV + 4 * z + 4] = t["conv_" + n][cols]
        hw[h, :, C_F2:C_F2 + P] = t["Wf2"][:, cols]
        hw[h, :, C_DT] = t["dt_bias"][cols]
        hw[h, :, C_AL] = t["A_log"][h]
        tw[h, :, C_G:C_WO] = tiles(t["Wg"][:, cols]).reshape(P, 256)
        tw[h, :, C_WO:C_BG] = t["Wo"][cols]
        tw[h, :, C_BG] = t["bg"][cols]
        tw[h, :, C_ON] = t["o_norm_w"]

    arrays = {
        "x": np.ascontiguousarray(t["hidden_states"].reshape(NT, P, D)),
        "gate_wT": np.ascontiguousarray(tiles(f["gate_weight"].T)),
        "expert_w": ew, "expert_scale": es, "route_w": rw, "shared_gu": sgu, "shared_down": sdn,
        "inv_map": np.ascontiguousarray(f["inv_mapping"].reshape(NE)),
        "head_w": hw, "tail_w": tw,
        "wf1": np.ascontiguousarray(tiles(t["Wf1"])),
        "wb": np.ascontiguousarray(tiles(t["Wb"])),
    }
    nc = bacc.Bacc("TRN2", target_bir_lowering=False, num_devices=1)
    args = [nc.dram_tensor(n, v.shape, mybir.dt.from_np(v.dtype), kind="ExternalInput").ap()
            for n, v in arrays.items()]
    out = nc.dram_tensor("out", (NT, P, D), mybir.dt.float32, kind="ExternalOutput").ap()
    macaron_kernel(nc, *args, out)
    r = run_bass_kernel_spmd(nc, [arrays], core_ids=[0])
    return r.results[0]["out"].reshape(NSEQ, T, D)
```

```python
import concourse.bass as bass
from concourse import mybir
from contextlib import ExitStack

P = 128
NSEQ, T, D = 4, 256, 256
NTOK = NSEQ * T
NT = NTOK // P
KT = D // P
H = 16
NE, F, K8, R = 64, 8, 8, 8
KR = K8 * R
I = 176
IR = I - P
ISH = 352
TOPK = 6
HALF = NTOK // 2
STEPS = 2 * F
ACCS = 2 * STEPS + 4
LEVELS = 7

C_GU, C_QA, C_QB, C_D1, C_D2, C_DQ, C_EW = 0, 768, 1024, 1408, 1664, 1920, 2176
C_KQV, C_F2, C_CONV, C_DT, C_AL, C_HW = 0, 768, 896, 908, 909, 910
C_G, C_WO, C_BG, C_ON, C_TW = 0, 256, 512, 513, 514

BEFORE = [["k0"], ["q0"], [], ["v0"], [], ["g0"], [], [], ["gt0"], ["sk0"], ["sq0", "sq1"], [],
          ["dg0", "dg1"], []]
AFTER = [["k1"], ["vt0"], ["q1"], ["vt1"], ["v1"], ["g1"], [], [], ["gt1"], ["sk1"], [], [], [], []]
TURN = [n for before, after in zip(BEFORE, AFTER) for n in before + after]
OWN = [n for n in TURN if n[:-1] in ("vt", "gt")]
NEXT = [n for n in TURN if n not in OWN]
assert len(TURN) % 2 == 0 and len(NEXT) % 2 == 0


def macaron_kernel(nc, x, gate_wT, expert_w, expert_scale, route_w, shared_gu, shared_down,
                   inv_map, head_w, tail_w, wf1, wb, out):
    f32 = mybir.dt.float32
    f32r = mybir.dt.float32r
    i32 = mybir.dt.int32
    u32 = mybir.dt.uint32
    ALU = mybir.AluOpType
    ACT = mybir.ActivationFunctionType
    AX = mybir.AxisListType

    ctx = ExitStack()
    with ctx:
        def sb(name, shape, dt=f32):
            return ctx.enter_context(nc.sbuf_tensor(name, shape, dt))

        def sem(name):
            return ctx.enter_context(nc.semaphore(name))

        x_res = sb("x_res", [P, NT, D])
        xnT = sb("xnT", [P, KT, NTOK])
        ident = sb("ident", [P, P])
        ones = sb("ones", [P, P])
        masks = sb("masks", [P, LEVELS, 64])
        eps_ln = sb("eps_ln", [P, 1])
        eps_l2 = sb("eps_l2", [P, 1])
        onehot = sb("onehot", [NE, NE])
        gwT = sb("gwT", [P, KT, NE])
        stats = sb("stats", [P, NT, 6])
        mv = sb("mv", [P, NT, 2])
        lnv = sb("lnv", [P, 4, NT])

        phase = ExitStack()
        phase.__enter__()

        def ph(name, *shape, dt=f32, parts=P):
            return phase.enter_context(nc.sbuf_tensor(name, [parts, *shape], dt))

        def split(name, *shape, parts=P):
            return (ph(name + "_h", *shape, dt=f32r, parts=parts), ph(name + "_l", *shape, dt=f32r, parts=parts))

        xn_ffn = ph("xn_ffn", NT, D)
        ew = [ph(f"ew{i}", C_EW) for i in range(2)]
        es = [ph(f"es{i}", 640) for i in range(2)]
        rw = [ph(f"rw{i}", 384, parts=NE) for i in range(2)]
        shw = ph("shw", KT, 2 * ISH)
        shd = ph("shd", 3, D)
        sco = ph("sco", NT, NE + 2)
        lgt = ph("lgt", NT, NE + 2)
        small = ph("small", 8, NT * K8)
        top8 = ph("top8", NT, 8)
        half_scal = ph("half_scal", F * NT)
        ewr = [split(f"ewr{i}", C_EW) for i in range(2)]
        rwr = [split(f"rwr{i}", 384, parts=NE) for i in range(2)]
        softT = split("softT", NTOK, parts=NE)
        xer = [split(f"xer{i}", KT, HALF) for i in range(2)]
        awr = split("awr", HALF)
        h1r = [split(f"h1r{i}", HALF) for i in range(2)]
        h2r = [split(f"h2r{i}", HALF) for i in range(2)]
        scratch = ph("scratch", 5632)
        spot = [0]

        def of_scratch(*shape, parts=P):
            n = 1
            for k in shape:
                n *= k
            v = scratch[0:parts, spot[0]:spot[0] + n]
            spot[0] += n
            return v.rearrange("p (a b) -> p a b", a=shape[0]) if len(shape) == 2 else v

        wd = of_scratch(NT, NE)
        flat = of_scratch(NT * F, K8)
        soft = of_scratch(NT * F, K8)
        wdT = of_scratch(NTOK, parts=NE)
        shs = [of_scratch(HALF) for _ in range(3)]
        shh = [of_scratch(HALF) for _ in range(3)]
        spot[0] = 0
        xe = of_scratch(KT, HALF)
        wes = [of_scratch(HALF) for _ in range(4)]
        aw = of_scratch(HALF)
        sg0, sg2 = of_scratch(HALF), of_scratch(HALF)
        h1, h2 = of_scratch(HALF), of_scratch(HALF)
        phase.__exit__(None, None, None)

        ARENA = 47600
        arena = sb("arena", [P, ARENA])

        def carve(*shape, parts=P):
            n = 1
            for k in shape:
                n *= k
            v = arena[0:parts, spot[0]:spot[0] + n]
            spot[0] += n
            assert spot[0] <= ARENA, spot[0]
            if len(shape) == 2:
                v = v.rearrange("p (a b) -> p a b", a=shape[0])
            elif len(shape) == 3:
                v = v.rearrange("p (a b c) -> p a b c", a=shape[0], b=shape[1])
            return v

        spot[0] = 0
        kq = carve(2, NT, P)
        xn_attn = arena[:, 0:NT * D].rearrange("p (n d) -> p n d", n=NT)
        hw = carve(C_HW)
        tw = carve(C_TW)
        wf1s = carve(KT, P)
        wbs = carve(KT, H)
        xfT = carve(NTOK)
        beta = carve(H, NT)
        ebeta = carve(NT, H)
        raw = carve(3, NSEQ, T + 3)
        acc = carve(3, NSEQ, T)
        kqs = carve(2, NTOK)
        vs = carve(NTOK)
        rn = carve(2, NTOK)
        zg, eg, ge = carve(NTOK), carve(NTOK), carve(NTOK)
        nega = carve(2)
        qk = carve(2, NTOK)
        prod = rn[:, 0, :]
        diag = carve(NT)
        kr = carve(NT, P)
        tot = [ge] + [carve(NT * P >> l) for l in range(1, LEVELS)]
        vw = carve(2, NT, P)
        aq = carve(NT, P)
        bt = [carve(NT, P) for _ in range(LEVELS)]
        pt = [carve(NT, P) for _ in range(LEVELS)]
        vtok = carve(NT, P)
        uu = carve(NT, P)
        krt = carve(NSEQ, P)
        state = carve(NSEQ, P)
        r1 = carve(NSEQ, P)
        oT = carve(NT, P)
        sqo = carve(NTOK)
        gate = carve(NT, P)

        pb = [ctx.enter_context(nc.psum_tensor(f"pb{i}", [P, 512], f32)) for i in range(8)]

        S = {n: sem(n) for n in (
            "x_in", "consts_in", "inv_in", "shared_in", "attn_in", "consts", "pid", "onehot_made",
            "pads_made", "zeros_pool", "zeros_dve",
            "ln_stats", "ln_mv", "ln_var", "ln_step", "ln_rs", "ln_rsqrt", "ln_xn", "ln_tr", "ln_ev",
            "rt_logits", "rt_shift", "rt_exp", "rt_wd", "rt_wdt_tr", "rt_wdt", "rt_flat", "rt_mshift",
            "rt_mexp", "rt_soft", "rt_soft_tr", "rt_chain",
            "sh_gate", "sh_up", "sh_silu", "sh_h", "sh_out",
            "ew_in0", "ew_in1", "rw_in0", "rw_in1", "scaled", "w_hi", "w_lo", "r_hi", "r_lo", "soft_hi", "soft_lo",
            "x_full", "we_full", "we_ev", "xe_made", "xe_hi", "xe_lo", "a_made", "aw_made", "aw_hi", "aw_lo",
            "h_hi", "h_lo",
            "gu_full", "silu_done", "h_made", "da_full", "daw_made", "out_full", "out_acc",
            "ffn_over", "attn_over", "stored",
            "beta_full", "beta_exp", "beta_step", "beta_made", "xf_full", "xf_ev",
            "head_in", "tail_in", "pj_full", "pj_free", "conv_tap", "silu_head", "sq_head", "g_step",
            "ea_made", "na_made", "sp_made", "ge_made", "rn_ln", "rn_made", "qk_made", "prod_made",
            "kr_set", "vw_set", "aq_set", "lvl_upd", "tot_made",
            "al_full", "masked", "p_full", "p_ev", "d_full", "vw_upd",
            "u0_full", "u0_ev", "krt_full", "krt_ev", "s_full", "s_ev", "o0_full", "o0_ev",
            "ks_full", "r1_made", "u1_full", "u1_ev", "o1_full", "o1_ev", "sqo_made", "n_full",
            "n_ln", "rno_made", "gm_made", "on_made", "wo_full", "wo_acc")}
        EW_IN = [S["ew_in0"], S["ew_in1"]]
        RW_IN = [S["rw_in0"], S["rw_in1"]]
        PIECES = ((C_GU, C_QA), (C_QA, C_D1), (C_D1, C_EW))

        def halves(ap, m, s):
            return ap.rearrange("p (n s m) -> p n s m", s=2, m=m)[:, :, s, :]

        def turn_base(h):
            return len(TURN) * h + len(NEXT)

        def own(name, h, last):
            return len(TURN) * h + (len(NEXT) + (OWN if last else TURN).index(name) + 1)

        T0, T1 = 4, 7

        block = ctx.enter_context(nc.Block())

        @block.sync
        def _(sp):
            sp.dma_start(x_res[:, 0:4, :], x[0:4].rearrange("n p d -> p n d")).then_inc(S["x_in"], 16)
            sp.dma_start(x_res[:, 4:8, :], x[4:8].rearrange("n p d -> p n d")).then_inc(S["x_in"], 16)
            sp.dma_start(gwT[:, :, :], gate_wT).then_inc(S["consts_in"], 16)
            sp.dma_start(small[0:NE, 0, :].bitcast(i32), inv_map.partition_broadcast(NE)).then_inc(S["inv_in"], 16)

            def ffn(q):
                def route(f, pf):
                    sp.dma_start(rw[pf][:, :], route_w[f]).then_inc(RW_IN[pf], 16)

                def group(f, pf):
                    sp.dma_start(ew[pf][:, :], expert_w[f]).then_inc(EW_IN[pf], 16)
                    sp.dma_start(es[pf][:, :], expert_scale[f].partition_broadcast(P)).then_inc(EW_IN[pf], 16)

                sp.dma_start(shw[:, :, :], shared_gu).then_inc(S["shared_in"], 16)
                sp.dma_start(shd[:, :, :], shared_down).then_inc(S["shared_in"], 16)
                for f in range(2):
                    route(f, f)
                    group(f, f)
                with sp.Fori(0, F // 2 - 1) as i:
                    for pf in range(2):
                        sp.wait_ge(S["r_lo"], 2 * i + (F * q + pf + 1))
                        route(bass.ds(2 * i + (2 + pf), 1), pf)
                        sp.wait_ge(S["w_lo"], 6 * i + 3 * (F * q + pf + 1))
                        group(bass.ds(2 * i + (2 + pf), 1), pf)

            ffn(0)
            sp.wait_ge(S["ffn_over"], 1)
            sp.dma_start(wf1s, wf1).then_inc(S["attn_in"], 16)
            sp.dma_start(wbs, wb).then_inc(S["attn_in"], 16)
            sp.dma_start(hw, head_w[0]).then_inc(S["head_in"], 16)
            sp.dma_start(tw, tail_w[0]).then_inc(S["tail_in"], 16)
            sp.wait_ge(S["silu_head"], 3)
            sp.dma_start(hw, head_w[1]).then_inc(S["head_in"], 16)
            sp.wait_ge(S["silu_head"], 6)
            sp.dma_start(hw, head_w[2]).then_inc(S["head_in"], 16)
            with sp.Fori(1, H - 2) as h:
                sp.wait_ge(S["wo_full"], 4 * h)
                sp.dma_start(tw, tail_w[bass.ds(h, 1)]).then_inc(S["tail_in"], 16)
                sp.wait_ge(S["silu_head"], 3 * h + 6)
                sp.dma_start(hw, head_w[bass.ds(h + 2, 1)]).then_inc(S["head_in"], 16)
            for h in range(H - 2, H):
                sp.wait_ge(S["wo_full"], 4 * h)
                sp.dma_start(tw, tail_w[h]).then_inc(S["tail_in"], 16)
            sp.wait_ge(S["attn_over"], 1)
            ffn(1)
            sp.wait_ge(S["ffn_over"], 2)
            sp.dma_start(out.rearrange("n p d -> p n d"), x_res[:, :, :]).then_inc(S["stored"], 16)
            sp.wait_ge(S["stored"], 16)

        @block.gpsimd
        def _(pool):
            nc.gpsimd.memset(ident[:, :], 0.0).then_inc(S["consts"], 1)
            nc.gpsimd.memset(ones[:, :], 1.0).then_inc(S["consts"], 1)
            nc.gpsimd.memset(masks[:, :, :], 1.0).then_inc(S["consts"], 1)
            nc.gpsimd.memset(eps_ln[:, :], 1e-5).then_inc(S["consts"], 1)
            nc.gpsimd.memset(eps_l2[:, :], 1e-6).then_inc(S["consts"], 1)
            nc.gpsimd.iota(small[0:NE, 1, 0:1].bitcast(i32), pattern=[[0, 1]], base=0,
                           channel_multiplier=1).then_inc(S["pid"], 1)
            nc.gpsimd.memset(sco[:, :, NE:NE + 2], -1.0).then_inc(S["pads_made"], 1)
            pool.wait_ge(S["consts"], 5)
            nc.gpsimd.affine_select(out=ident[:, :], in_=ident[:, :], compare_op=ALU.not_equal, fill=1.0,
                                    base=0, pattern=[[-1, P]], channel_multiplier=1).then_inc(S["consts"], 1)
            for l in range(LEVELS):
                m = 1 << l
                mk = masks[:, l, :].rearrange("p (n m) -> p n m", m=m)
                nc.gpsimd.affine_select(out=mk, in_=mk, compare_op=ALU.is_ge, fill=0.0, base=0,
                                        pattern=[[-2 * m, 64 // m], [0, m]],
                                        channel_multiplier=1).then_inc(S["consts"], 1)
                pool.wait_ge(S["consts"], 7 + 2 * l)
                nc.gpsimd.affine_select(out=mk, in_=mk, compare_op=ALU.is_ge, fill=0.0, base=m - 1,
                                        pattern=[[2 * m, 64 // m], [0, m]],
                                        channel_multiplier=-1).then_inc(S["consts"], 1)

            def ffn(q):
                def rest(out, whole, high):
                    return nc.gpsimd.tensor_tensor(out, whole, high.bitcast(f32), ALU.subtract)

                def split_route(gf, pf):
                    pool.wait_ge(S["r_hi"], gf + 1)
                    rest(rwr[pf][1][:, :], rw[pf][:, :], rwr[pf][0][:, :]).then_inc(S["r_lo"], 1)

                def split_group(gf, pf):
                    for n, (a, b) in enumerate(PIECES):
                        pool.wait_ge(S["w_hi"], 3 * gf + (n + 1))
                        rest(ewr[pf][1][:, a:b], ew[pf][:, a:b], ewr[pf][0][:, a:b]).then_inc(S["w_lo"], 1)

                def split_xe(g, par):
                    pool.wait_ge(S["xe_hi"], g + 1)
                    rest(xer[par][1][:, :, :], xe, xer[par][0][:, :, :]).then_inc(S["xe_lo"], 1)

                def split_aw(g):
                    pool.wait_ge(S["aw_hi"], g + 1)
                    rest(awr[1][:, :], aw, awr[0][:, :]).then_inc(S["aw_lo"], 1)

                def step(g, gf, j, left):
                    pf, hh = j // 2, j % 2
                    if left > 2:
                        split_xe(g + 2, hh)
                    if left > 1:
                        split_aw(g + 1)
                    if hh == 0 and left > 2:
                        split_group(gf + 1, 1 - pf)
                    if hh == 1 and left > 4:
                        split_route(gf + 2, pf)

                split_route(F * q, 0)
                split_group(F * q, 0)
                split_route(F * q + 1, 1)
                split_xe(STEPS * q, 0)
                split_xe(STEPS * q + 1, 1)
                split_aw(STEPS * q)
                with pool.Fori(0, F // 2 - 1) as i:
                    for j in range(4):
                        step(4 * i + (STEPS * q + j), 2 * i + (F * q + j // 2), j, STEPS)
                for j in range(4):
                    step(STEPS * (q + 1) - 4 + j, F * (q + 1) - 2 + j // 2, j, 4 - j)

            ffn(0)
            pool.wait_ge(S["ffn_over"], 1)
            for l in range(LEVELS):
                nc.gpsimd.memset(bt[l], 0.0).then_inc(S["zeros_pool"], 1)

            def set_w(h, g, t, fresh):
                if not fresh:
                    pool.wait_ge(S["u1_full"], t - 1)
                nc.gpsimd.tensor_tensor(
                    vw[:, :, 4 * g:4 * g + 4, :],
                    ident[:, :].unsqueeze(1).unsqueeze(1).broadcast_to([P, 2, 4, P]),
                    beta[:, bass.ds(h, 1), 4 * g:4 * g + 4].broadcast_to([P, 2, 4])
                    .unsqueeze(3).broadcast_to([P, 2, 4, P]), ALU.mult).then_inc(S["vw_set"], 1)

            def set_diagonal(h, g, t, fresh):
                pool.wait_ge(S["pj_free"], turn_base(h))
                if not fresh:
                    pool.wait_ge(S["o1_full"], t - 1)
                nc.gpsimd.tensor_tensor(
                    aq[:, 4 * g:4 * g + 4, :], ident[:, :].unsqueeze(1).broadcast_to([P, 4, P]),
                    diag[:, 4 * g:4 * g + 4].unsqueeze(2).broadcast_to([P, 4, P]), ALU.mult).then_inc(S["aq_set"], 1)

            def level(l, g, t):
                m = 1 << l
                nb = 4 * 64 // m
                pool.wait_ge(S["al_full"], 7 * t + l + 1)
                if l == 0:
                    pool.wait_ge(S["kr_set"], t + 1)
                else:
                    pool.wait_ge(S["tot_made"], 6 * t + l)
                    pool.wait_ge(S["lvl_upd"], 14 * t + 2 * l)
                n = 4 * P >> l
                t2 = tot[l][:, g * n:(g + 1) * n].rearrange("p (b s) -> p b s", s=2)
                k2 = kq[:, :, 4 * g:4 * g + 4, :].rearrange("p z u t -> p z (u t)")
                k2 = k2.rearrange("p z (b s m) -> p z b s m", s=2, m=m)[:, :, :, 1, :]
                nc.gpsimd.tensor_tensor(
                    k2, k2, t2[:, :, 0].unsqueeze(1).unsqueeze(3).broadcast_to([P, 2, nb, m]),
                    ALU.mult).then_inc(S["lvl_upd"], 1)
                r2 = kr[:, 4 * g:4 * g + 4, :].rearrange("p u t -> p (u t)")
                r2 = r2.rearrange("p (b s m) -> p b s m", s=2, m=m)[:, :, 0, :]
                nc.gpsimd.tensor_tensor(
                    r2, r2, t2[:, :, 1].unsqueeze(2).broadcast_to([P, nb, m]),
                    ALU.mult).then_inc(S["lvl_upd"], 1)
                if l < LEVELS - 1:
                    nc.gpsimd.tensor_tensor(tot[l + 1][:, g * n // 2:(g + 1) * n // 2], t2[:, :, 0],
                                            t2[:, :, 1], ALU.mult).then_inc(S["tot_made"], 1)

            def multiply(hp):
                pool.wait_ge(S["qk_made"], 2 * hp + 2)
                nc.gpsimd.tensor_tensor(prod, qk[:, 0, :], qk[:, 1, :], ALU.mult).then_inc(S["prod_made"], 1)

            def turn(h, first, prep):
                for s in range(14):
                    g, l = s // LEVELS, s % LEVELS
                    level(l, g, 2 * h + g)
                    if s == 5:
                        set_w(h, 1, 2 * h + 1, first)
                        set_diagonal(h, 1, 2 * h + 1, first)
                    if s == 11 and prep:
                        set_w(h + 1, 0, 2 * h + 2, False)
                        multiply(h + 1)
                    if s == 12 and prep:
                        set_diagonal(h + 1, 0, 2 * h + 2, False)

            pool.wait_ge(S["beta_made"], 1)
            set_w(0, 0, 0, True)
            multiply(0)
            set_diagonal(0, 0, 0, True)
            turn(0, True, True)
            with pool.Fori(1, H - 1) as h:
                turn(h, False, True)
            turn(H - 1, False, False)
            pool.wait_ge(S["attn_over"], 1)
            ffn(1)

        @block.scalar
        def _(act):
            act.wait_ge(S["consts"], 6 + 2 * LEVELS)

            def layernorm(k):
                act.wait_ge(S["ln_var"], k + 1)
                nc.scalar.activation(lnv[:, 1, :], lnv[:, 0, :], ACT.Ln).then_inc(S["ln_step"], 1)
                act.wait_ge(S["ln_step"], k + 1)
                nc.scalar.activation(lnv[:, 1, :], lnv[:, 1, :], ACT.Exp, scale=-0.5).then_inc(S["ln_rs"], 1)
                for j in range(4):
                    act.wait_ge(S["ln_tr"], 4 * k + j + 1)
                    nc.scalar.copy(xnT[:, :, j * 256:(j + 1) * 256],
                                   pb[j % 2][:, :].rearrange("p (k t) -> p k t", k=KT)).then_inc(S["ln_ev"], 1)

            def ffn(q):
                layernorm(2 * q)
                act.wait_ge(S["rt_shift"], q + 1)
                nc.scalar.activation(lgt[:, :, 0:NE], lgt[:, :, 0:NE], ACT.Exp).then_inc(S["rt_exp"], 1)

                def shared(hh):
                    for m in range(3):
                        mw = min(P, ISH - m * P)
                        act.wait_ge(S["sh_gate"], 6 * q + 3 * hh + m + 1)
                        nc.scalar.activation(shs[m][0:mw], pb[2 * m][0:mw, :], ACT.Silu).then_inc(S["sh_silu"], 1)

                shared(0)
                for j in range(2):
                    act.wait_ge(S["rt_wdt_tr"], 2 * q + j + 1)
                    nc.scalar.copy(wdT[:, j * 512:(j + 1) * 512], pb[j][0:NE, :]).then_inc(S["rt_wdt"], 1)
                act.wait_ge(S["rt_mshift"], q + 1)
                nc.scalar.activation(soft, soft, ACT.Exp).then_inc(S["rt_mexp"], 1)
                shared(1)
                def split_route(gf, n, pf):
                    act.wait_ge(RW_IN[pf], n)
                    nc.scalar.copy(rwr[pf][0][:, :], rw[pf][:, :]).then_inc(S["r_hi"], 1)

                def split_group(gf, pf, first):
                    act.wait_ge(S["scaled"], gf + 1)
                    if not first:
                        act.wait_ge(S["out_full"], 4 * gf - 4)
                    for a, b in PIECES:
                        nc.scalar.copy(ewr[pf][0][:, a:b], ew[pf][:, a:b]).then_inc(S["w_hi"], 1)

                def spread(g, j):
                    act.wait_ge(S["we_full"], g + 1)
                    nc.scalar.copy(wes[j], pb[2][:, :]).then_inc(S["we_ev"], 1)

                def split_xe(g, par):
                    act.wait_ge(S["xe_made"], g + 1)
                    nc.scalar.copy(xer[par][0][:, :, :], xe).then_inc(S["xe_hi"], 1)

                def split_aw(g):
                    act.wait_ge(S["aw_made"], g + 1)
                    nc.scalar.copy(awr[0][:, :], aw).then_inc(S["aw_hi"], 1)

                def step(g, gf, i, j, left):
                    pf, hh = j // 2, j % 2
                    act.wait_ge(S["gu_full"], 3 * g + 1)
                    nc.scalar.activation(sg0, pb[4][:, :], ACT.Silu).then_inc(S["silu_done"], 1)
                    act.wait_ge(S["gu_full"], 3 * g + 3)
                    nc.scalar.activation(sg2[0:64], pb[6][0:64, :], ACT.Silu).then_inc(S["silu_done"], 1)
                    act.wait_ge(S["h_made"], 2 * g + 1)
                    nc.scalar.copy(h1r[hh][0][:, :], h1).then_inc(S["h_hi"], 1)
                    act.wait_ge(S["h_made"], 2 * g + 2)
                    nc.scalar.copy(h2r[hh][0][0:64, :], h2[0:64]).then_inc(S["h_hi"], 1)
                    if left > 2:
                        spread(g + 2, (j + 2) % 4)
                        split_xe(g + 2, hh)
                    if left > 1:
                        split_aw(g + 1)
                    act.wait_ge(S["daw_made"], g + 1)
                    nc.scalar.copy(h2r[hh][0][64:P, :], h2[64:P]).then_inc(S["h_hi"], 1)
                    if hh == 0 and left > 2:
                        split_group(gf + 1, 1 - pf, False)
                    if hh == 1 and left > 4:
                        split_route(gf + 2, 16 * i + 16 * (4 * q + 2), pf)

                split_route(F * q, 16 * (4 * q + 1), 0)
                split_group(F * q, 0, True)
                split_route(F * q + 1, 16 * (4 * q + 1), 1)
                for j in range(2):
                    act.wait_ge(S["rt_soft_tr"], 2 * q + j + 1)
                    nc.scalar.copy(softT[0][:, j * 512:(j + 1) * 512], pb[j][0:NE, :]).then_inc(S["soft_hi"], 1)
                for j in range(2):
                    spread(STEPS * q + j, j)
                    split_xe(STEPS * q + j, j)
                split_aw(STEPS * q)
                with act.Fori(0, F // 2 - 1) as i:
                    for j in range(4):
                        step(4 * i + (STEPS * q + j), 2 * i + (F * q + j // 2), i, j, STEPS)
                for j in range(4):
                    step(STEPS * (q + 1) - 4 + j, F * (q + 1) - 2 + j // 2, F // 2 - 1, j, 4 - j)

            ffn(0)
            act.wait_ge(S["ffn_over"], 1)
            layernorm(1)
            act.wait_ge(S["beta_full"], 1)
            nc.scalar.activation(ebeta, pb[4][:, 0:NT * H].rearrange("p (n h) -> p n h", n=NT),
                                 ACT.Exp, scale=-1.0).then_inc(S["beta_exp"], 1)
            for hh in range(2):
                act.wait_ge(S["xf_full"], hh + 1)
                nc.scalar.copy(xfT[:, hh * HALF:(hh + 1) * HALF], pb[5 + hh][:, :]).then_inc(S["xf_ev"], 1)
            act.wait_ge(S["zeros_dve"], LEVELS + 1)

            def half(ap, hh):
                return ap[:, hh * HALF:(hh + 1) * HALF]

            def units(bank):
                return bank[:, 0:2 * P].rearrange("p (u t) -> p u t", u=2)

            def chunk(buf, g, c):
                return buf[:, 4 * g:4 * g + 4, :].rearrange("p (s c) t -> p s c t", c=2)[:, :, c, :]

            def tail(s, g, t):
                if s == 0:
                    act.wait_ge(S["u0_full"], t + 1)
                    nc.scalar.copy(chunk(uu, g, 0), units(pb[T0])).then_inc(S["u0_ev"], 1)
                    act.wait_ge(S["krt_full"], t + 1)
                    nc.scalar.copy(krt[:, 2 * g:2 * g + 2, :], units(pb[T1])).then_inc(S["krt_ev"], 1)
                if s == 1:
                    act.wait_ge(S["o0_full"], t + 1)
                    nc.scalar.copy(chunk(oT, g, 0), units(pb[T1])).then_inc(S["o0_ev"], 1)
                if s == 3:
                    act.wait_ge(S["u1_full"], t + 1)
                    nc.scalar.copy(chunk(uu, g, 1), units(pb[T1])).then_inc(S["u1_ev"], 1)
                if s == 4:
                    act.wait_ge(S["o1_full"], t + 1)
                    nc.scalar.copy(chunk(oT, g, 1), units(pb[T0])).then_inc(S["o1_ev"], 1)
                    act.wait_ge(S["o1_ev"], t + 1)
                    nc.scalar.activation(half(sqo, g), oT[:, 4 * g:4 * g + 4, :].rearrange("p u t -> p (u t)"),
                                         ACT.Square).then_inc(S["sqo_made"], 1)
                if s == 5:
                    act.wait_ge(S["n_full"], t + 1)
                    nc.scalar.activation(half(sqo, g), pb[T1][:, :], ACT.Ln, bias=eps_ln[:, :],
                                         scale=1.0 / P).then_inc(S["n_ln"], 1)
                    act.wait_ge(S["n_ln"], t + 1)
                    nc.scalar.activation(half(sqo, g), half(sqo, g), ACT.Exp, scale=-0.5).then_inc(S["rno_made"], 1)

            def turn(h, hp, first, delta, prep):
                names = TURN if delta and prep else (NEXT if prep else OWN)
                base = turn_base(h) if delta else 0

                def arrive(name):
                    act.wait_ge(S["pj_full"], base + (names.index(name) + 1))
                    return pb[5 + names.index(name) % 2]

                def evacuate(name):
                    kind, hh = name[:-1], int(name[-1])
                    if kind in ("k", "q", "v"):
                        z = ("k", "q", "v").index(kind)
                        if name == "k0":
                            act.wait_ge(S["head_in"], 16 * hp + 16)
                        seqs = arrive(name)[:, :].rearrange("p (s t) -> p s t", s=2)
                        nc.scalar.copy(raw[:, z, 2 * hh:2 * hh + 2, 3:3 + T], seqs)
                        nc.scalar.activation(acc[:, z, 2 * hh:2 * hh + 2, :], seqs, ACT.Copy,
                                             scale=hw[:, C_CONV + 4 * z + 3:C_CONV + 4 * z + 4]
                                             ).then_inc(S["pj_free"], 1)
                    elif kind == "vt":
                        if not first:
                            act.wait_ge(S["r1_made"], 2 * h + (hh - 1))
                        nc.scalar.copy(vtok[:, 4 * hh:4 * hh + 4, :],
                                       arrive(name)[:, :].rearrange("p (u t) -> p u t", u=4)).then_inc(S["pj_free"], 1)
                    elif kind == "g":
                        nc.scalar.activation(half(zg, hh), arrive(name)[:, :], ACT.Identity,
                                             bias=hw[:, C_DT:C_DT + 1]).then_inc(S["pj_free"], 1)
                    elif kind == "gt":
                        if hh == 0:
                            act.wait_ge(S["tail_in"], 16 * h + 16)
                        if not first:
                            act.wait_ge(S["wo_full"], 4 * h + 2 * (hh - 1))
                        nc.scalar.activation(gate[:, 4 * hh:4 * hh + 4, :],
                                             arrive(name)[:, :].rearrange("p (u t) -> p u t", u=4), ACT.Silu,
                                             bias=tw[:, C_BG:C_BG + 1]).then_inc(S["pj_free"], 1)
                    elif kind in ("sk", "sq"):
                        z = ("sk", "sq").index(kind)
                        nc.scalar.activation(half(rn[:, z, :], hh), arrive(name)[:, :], ACT.Ln,
                                             bias=eps_l2[:, :]).then_inc(S["pj_free"], 1)
                        if hh == 1:
                            act.wait_ge(S["pj_free"], base + (names.index(name) + 1))
                            nc.scalar.activation(rn[:, z, :], rn[:, z, :], ACT.Exp, scale=-0.5).then_inc(S["rn_made"], 1)
                    else:
                        nc.scalar.copy(diag[:, 4 * hh:4 * hh + 4], 
                                       arrive(name)[:, 0:256].rearrange("p (u n) -> p u n", u=4)[:, :, 0]).then_inc(S["pj_free"], 1)

                def silu(z, target):
                    act.wait_ge(S["conv_tap"], 18 * hp + 6 * z + 6)
                    nc.scalar.activation(target, acc[:, z].rearrange("p s t -> p (s t)"),
                                         ACT.Silu).then_inc(S["silu_head"], 1)

                def square(z):
                    act.wait_ge(S["silu_head"], 3 * hp + z + 1)
                    nc.scalar.activation(acc[:, z].rearrange("p s t -> p (s t)"), kqs[:, z, :],
                                         ACT.Square).then_inc(S["sq_head"], 1)

                for s in range(14):
                    g, l = s // LEVELS, s % LEVELS
                    t = 2 * h + g if delta else None
                    if delta:
                        m = 1 << l
                        act.wait_ge(S["p_full"], 7 * t + l + 1)
                        nc.scalar.copy(
                            halves(pt[l][:, 4 * g:4 * g + 4, :].rearrange("p u t -> p (u t)"), m, 0),
                            pb[2][:, 0:256].rearrange("p (n m) -> p n m", m=m)).then_inc(S["p_ev"], 1)
                    if s == 6 and prep:
                        nc.scalar.activation(nega[:, 0:1], hw[:, C_AL:C_AL + 1], ACT.Exp).then_inc(S["ea_made"], 1)
                    if s == 7:
                        act.preload_act_table_set("silu_and_others")
                    if s == 9:
                        act.preload_act_table_set("natural_log_exp_and_others")
                    for name in BEFORE[s]:
                        if name in names:
                            evacuate(name)
                    if delta and not (first and g == 0):
                        tail(l, 1 - g, t - 1)
                    if s == 6 and prep:
                        act.wait_ge(S["pj_free"], base + (names.index("g1") + 1))
                        nc.scalar.activation(eg, zg, ACT.Abs).then_inc(S["g_step"], 1)
                        act.wait_ge(S["g_step"], 3 * hp + 1)
                        nc.scalar.activation(eg, eg, ACT.Exp, scale=-1.0).then_inc(S["g_step"], 1)
                        act.wait_ge(S["g_step"], 3 * hp + 2)
                        nc.scalar.activation(eg, eg, ACT.Ln, bias=1.0).then_inc(S["g_step"], 1)
                    if s == 7 and prep:
                        silu(0, kqs[:, 0, :])
                        silu(1, kqs[:, 1, :])
                        square(0)
                    if s == 8 and prep:
                        square(1)
                        silu(2, vs)
                    if s == 10 and prep:
                        act.wait_ge(S["sp_made"], hp + 1)
                        act.wait_ge(S["na_made"], hp + 1)
                        if delta:
                            act.wait_ge(S["tot_made"], 12 * h + 7)
                        nc.scalar.activation(ge, zg, ACT.Exp, scale=nega[:, 1:2]).then_inc(S["ge_made"], 1)
                    for name in AFTER[s]:
                        if name in names:
                            evacuate(name)

            act.preload_act_table_set("natural_log_exp_and_others")
            turn(None, 0, False, False, True)
            turn(0, 1, True, True, True)
            with act.Fori(1, H - 1) as h:
                turn(h, h + 1, False, True, True)
            turn(H - 1, None, False, True, False)
            for s in range(LEVELS):
                tail(s, 1, 2 * H - 1)
            act.wait_ge(S["attn_over"], 1)
            ffn(1)

        @block.vector
        def _(dve):
            V = nc.vector
            chain = [0]

            def link(ins):
                chain[0] += 1
                ins.then_inc(S["rt_chain"], 1)
                dve.wait_ge(S["rt_chain"], chain[0])

            inv_f, neg_f, pid_f = small[0:NE, 2, :], small[0:NE, 3, :], small[0:NE, 4, 0:1]
            dve.wait_ge(S["inv_in"], 16)
            dve.wait_ge(S["pid"], 1)
            V.tensor_copy(inv_f, small[0:NE, 0, :].bitcast(i32))
            link(V.tensor_copy(pid_f, small[0:NE, 1, 0:1].bitcast(i32)))
            link(V.tensor_scalar(neg_f, inv_f, 0.0, float(NE), ALU.is_lt, ALU.mult))
            link(V.tensor_tensor(inv_f, inv_f, neg_f, ALU.add))
            link(V.tensor_scalar(inv_f, inv_f, 0.0, float(NE - 1), ALU.max, ALU.min))
            V.tensor_scalar(onehot[:, :], inv_f, pid_f, None, ALU.is_equal).then_inc(S["onehot_made"], 1)
            dve.wait_ge(S["pads_made"], 1)

            def layernorm(k):
                for n in range(NT):
                    V.bn_stats(stats[:, n, :], x_res[:, n, :]).then_inc(S["ln_stats"], 1)
                dve.wait_ge(S["ln_stats"], NT * (k + 1))
                for n in range(NT):
                    last = V.bn_aggr(mv[:, n, :], stats[:, n, :])
                link(last)
                var, y, t = lnv[:, 0, :], lnv[:, 1, :], lnv[:, 2, :]
                V.tensor_scalar(var, mv[:, :, 1], 1e-5, None, ALU.add).then_inc(S["ln_var"], 1)
                dve.wait_ge(S["ln_rs"], k + 1)
                dve.wait_ge(S["ln_var"], k + 1)
                link(V.tensor_tensor(t, var, y, ALU.mult))
                link(V.tensor_tensor(t, t, y, ALU.mult))
                link(V.tensor_scalar(t, t, -0.5, 1.5, ALU.mult, ALU.add))
                link(V.tensor_tensor(lnv[:, 3, :], y, t, ALU.mult))
                for n in range(NT):
                    V.tensor_scalar((xn_attn if k == 1 else xn_ffn)[:, n, :], x_res[:, n, :], mv[:, n, 0:1], lnv[:, 3, n:n + 1],
                                    ALU.subtract, ALU.mult).then_inc(S["ln_xn"], 1)

            def ffn(q):
                layernorm(2 * q)
                if q == 1:
                    link(V.memset(sco[:, :, NE:NE + 2], -1.0))
                mx, sm = small[:, 0, 0:NT], small[:, 1, 0:NT]
                dve.wait_ge(S["rt_logits"], q + 1)
                lg = pb[7][:, :].rearrange("p (n e) -> p n e", n=NT)
                link(V.reduce_max(mx, lg, AX.X))
                V.tensor_tensor(lgt[:, :, 0:NE], lg, mx.unsqueeze(2).broadcast_to([P, NT, NE]),
                                ALU.subtract).then_inc(S["rt_shift"], 1)
                dve.wait_ge(S["rt_exp"], q + 1)
                link(V.reduce_sum(sm, lgt[:, :, 0:NE], AX.X))
                link(V.reciprocal(sm, sm))
                link(V.tensor_tensor(sco[:, :, 0:NE], lgt[:, :, 0:NE],
                                     sm.unsqueeze(2).broadcast_to([P, NT, NE]), ALU.mult))
                for n in range(NT):
                    last = V.max(top8[:, n, :], sco[:, n, 0:NE])
                link(last)
                link(V.memset(top8[:, :, TOPK:8], -1.0))
                for n in range(NT):
                    last = V.match_replace(lgt[:, n, :], top8[:, n, :], sco[:, n, :], 0.0)
                link(last)
                V.tensor_tensor(wd, sco[:, :, 0:NE], lgt[:, :, 0:NE], ALU.subtract).then_inc(S["rt_wd"], 1)

                def shared(hh):
                    for m in range(3):
                        mw = min(P, ISH - m * P)
                        dve.wait_ge(S["sh_silu"], 6 * q + 3 * hh + m + 1)
                        dve.wait_ge(S["sh_up"], 6 * q + 3 * hh + m + 1)
                        V.tensor_tensor(shh[m][0:mw], shs[m][0:mw], pb[2 * m + 1][0:mw, :],
                                        ALU.mult).then_inc(S["sh_h"], 1)
                    for j in range(2):
                        dve.wait_ge(S["sh_out"], 4 * q + 2 * hh + j + 1)
                        xv = x_res[:, 4 * hh + 2 * j:4 * hh + 2 * j + 2, :].rearrange("p n d -> p (n d)")
                        V.scalar_tensor_tensor(out=xv, in0=pb[6 + j][:, :], scalar=0.5, in1=xv,
                                               op0=ALU.mult, op1=ALU.add).then_inc(S["out_acc"], 1)

                shared(0)
                dve.wait_ge(S["rt_flat"], q + 1)
                link(V.tensor_copy(flat, pb[2][:, :].rearrange("p (a k) -> p a k", k=K8)))
                sums, mk = small[:, 2, :], small[:, 3, :]
                link(V.reduce_sum(sums, flat, AX.X))
                V.tensor_scalar(half_scal.rearrange("p (f n) -> p n f", f=F),
                                sums.rearrange("p (n f) -> p n f", n=NT), 0.5, None, ALU.mult)
                link(V.tensor_scalar(soft, flat, 0.0, -1e9, ALU.is_equal, ALU.mult))
                link(V.tensor_tensor(soft, soft, flat, ALU.add))
                link(V.reduce_max(mk, soft, AX.X))
                V.tensor_tensor(soft, soft, mk.unsqueeze(2).broadcast_to([P, NT * F, K8]),
                                ALU.subtract).then_inc(S["rt_mshift"], 1)
                dve.wait_ge(S["rt_mexp"], q + 1)
                link(V.reduce_sum(mk, soft, AX.X))
                link(V.reciprocal(mk, mk))
                V.tensor_tensor(soft, soft, mk.unsqueeze(2).broadcast_to([P, NT * F, K8]),
                                ALU.mult).then_inc(S["rt_soft"], 1)

                def scale_weights(n, pf):
                    dve.wait_ge(EW_IN[pf], n)
                    V.tensor_tensor(ew[pf][:, C_QB:C_D1], ew[pf][:, C_QB:C_D1], es[pf][:, 0:384], ALU.mult)
                    V.tensor_tensor(ew[pf][64:P, C_D2:C_DQ], ew[pf][64:P, C_D2:C_DQ],
                                    es[pf][64:P, 384:640], ALU.mult).then_inc(S["scaled"], 1)

                def add_w(g, par, fresh):
                    dve.wait_ge(S["x_full"], g + 1)
                    if not fresh:
                        dve.wait_ge(S["xe_lo"], g)
                    for kt in range(KT):
                        last = V.tensor_tensor(xe[:, kt, :], pb[kt][:, :],
                                               xnT[:, kt, par * HALF:(par + 1) * HALF], ALU.add)
                    last.then_inc(S["xe_made"], 1)

                def weigh(g, j, fresh):
                    dve.wait_ge(S["a_made"], g + 1)
                    dve.wait_ge(S["we_ev"], g + 1)
                    if not fresh:
                        dve.wait_ge(S["aw_lo"], g)
                    V.tensor_tensor(aw, pb[3][:, :], wes[j], ALU.mult).then_inc(S["aw_made"], 1)

                def rest(out, whole, high):
                    V.tensor_tensor(out, whole, high.bitcast(f32), ALU.subtract).then_inc(S["h_lo"], 1)

                def step(g, i, j, left):
                    pf, hh = j // 2, j % 2
                    dve.wait_ge(S["silu_done"], 2 * g + 1)
                    dve.wait_ge(S["gu_full"], 3 * g + 2)
                    V.tensor_tensor(h1, sg0, pb[5][:, :], ALU.mult).then_inc(S["h_made"], 1)
                    dve.wait_ge(S["silu_done"], 2 * g + 2)
                    V.tensor_tensor(h2[0:64], sg2[0:64], pb[6][64:P, :], ALU.mult).then_inc(S["h_made"], 1)
                    dve.wait_ge(S["h_hi"], 3 * g + 1)
                    rest(h1r[hh][1][:, :], h1, h1r[hh][0][:, :])
                    dve.wait_ge(S["h_hi"], 3 * g + 2)
                    rest(h2r[hh][1][0:64, :], h2[0:64], h2r[hh][0][0:64, :])
                    if left > 2:
                        add_w(g + 2, hh, False)
                    if left > 1:
                        weigh(g + 1, (j + 1) % 4, False)
                    dve.wait_ge(S["da_full"], g + 1)
                    V.tensor_tensor(h2[64:P], pb[7][64:P, :], wes[j][64:P], ALU.mult).then_inc(S["daw_made"], 1)
                    dve.wait_ge(S["h_hi"], 3 * g + 3)
                    rest(h2r[hh][1][64:P, :], h2[64:P], h2r[hh][0][64:P, :])
                    if hh == 1 and left > 4:
                        scale_weights(32 * i + 32 * (4 * q + 2), pf)
                    for k in range(2):
                        dve.wait_ge(S["out_full"], 2 * g + k + 1)
                        for t in range(2):
                            n = 4 * hh + 2 * k + t
                            acc_op = V.scalar_tensor_tensor(
                                out=x_res[:, n, :], in0=pb[5 + k][:, t * D:(t + 1) * D],
                                scalar=half_scal[:, bass.ds(2 * NT * i + (pf * NT + n), 1)],
                                in1=x_res[:, n, :], op0=ALU.mult, op1=ALU.add)
                        acc_op.then_inc(S["out_acc"], 1)

                scale_weights(32 * (4 * q + 1), 0)
                scale_weights(32 * (4 * q + 1), 1)
                shared(1)
                for j in range(2):
                    dve.wait_ge(S["soft_hi"], 2 * q + j + 1)
                    V.tensor_tensor(softT[1][:, j * 512:(j + 1) * 512], pb[j][0:NE, :],
                                    softT[0][:, j * 512:(j + 1) * 512].bitcast(f32), ALU.subtract).then_inc(S["soft_lo"], 1)
                for j in range(2):
                    add_w(STEPS * q + j, j, q + j == 0)
                weigh(STEPS * q, 0, q == 0)
                with dve.Fori(0, F // 2 - 1) as i:
                    for j in range(4):
                        step(4 * i + (STEPS * q + j), i, j, STEPS)
                for j in range(4):
                    step(STEPS * (q + 1) - 4 + j, F // 2 - 1, j, 4 - j)
                dve.wait_ge(S["out_acc"], ACCS * (q + 1))
                V.tensor_copy(lnv[:, 2, 0:1], x_res[:, 0, 0:1]).then_inc(S["ffn_over"], 1)

            dve.wait_ge(S["x_in"], 32)
            ffn(0)
            dve.wait_ge(S["ffn_over"], 1)
            for l in range(LEVELS):
                V.memset(pt[l], 0.0).then_inc(S["zeros_dve"], 1)
            V.memset(raw[:, :, :, 0:3].rearrange("p z s t -> p (z s) t"), 0.0).then_inc(S["zeros_dve"], 1)
            layernorm(1)
            dve.wait_ge(S["beta_exp"], 1)
            link(V.tensor_scalar(ebeta, ebeta, 1.0, None, ALU.add))
            V.reciprocal(beta, ebeta.rearrange("p n h -> p h n")).then_inc(S["beta_made"], 1)
            dve.wait_ge(S["zeros_pool"], LEVELS)

            def set_up(h, g, t, fresh):
                cols = slice(g * HALF, (g + 1) * HALF)
                dve.wait_ge(S["qk_made"], 2 * h + 2)
                dve.wait_ge(S["ge_made"], h + 1)
                if not fresh:
                    dve.wait_ge(S["o1_full"], t - 1)
                V.tensor_tensor(kq[:, :, 4 * g:4 * g + 4, :].rearrange("p z u t -> p z (u t)"), qk[:, :, cols],
                                ge[:, cols].unsqueeze(1).broadcast_to([P, 2, HALF]), ALU.mult)
                V.tensor_copy(kr[:, 4 * g:4 * g + 4, :].rearrange("p u t -> p (u t)"),
                              qk[:, 0, cols]).then_inc(S["kr_set"], 1)

            def mask(l, g, t):
                m = 1 << l
                mk = masks[:, l, :].rearrange("p (n m) -> p n m", m=m).unsqueeze(1).broadcast_to([P, 4, 64 // m, m])
                bank = pb[(l + g) % 2][:, :].rearrange("p (u z n m) -> p u z n m", u=4, z=2, m=m)

                def second(buf):
                    return buf[:, 4 * g:4 * g + 4, :].rearrange("p u (n s m) -> p u n s m", s=2, m=m)[:, :, :, 1, :]

                if l == 0:
                    dve.wait_ge(S["aq_set"], t + 1)
                else:
                    dve.wait_ge(S["masked"], 14 * t + 2 * l)
                dve.wait_ge(S["al_full"], 7 * t + l + 1)
                V.tensor_tensor(second(bt[l]), bank[:, :, 0], mk, ALU.mult).then_inc(S["masked"], 1)
                V.copy_predicated(second(aq), mk.bitcast(u32), bank[:, :, 1]).then_inc(S["masked"], 1)

            def grow(l, g, t):
                m = 1 << l
                dve.wait_ge(S["d_full"], 7 * t + l + 1)
                if l == 0:
                    dve.wait_ge(S["vw_set"], t + 1)
                for z in ((1, 0) if l < LEVELS - 1 else (0,)):
                    part = vw[:, z, 4 * g:4 * g + 4, :].rearrange("p u (n s m) -> p (u n) s m", s=2, m=m)[:, :, 1 - z, :]
                    V.tensor_tensor(part, part, pb[3][:, z * 256:(z + 1) * 256].rearrange("p (n m) -> p n m", m=m),
                                    ALU.subtract).then_inc(S["vw_upd"], 1)

            def tail(s, g, t):
                def two(bank):
                    return bank[:, 0:2 * P].rearrange("p (u t) -> p u t", u=2)

                if s == 1:
                    dve.wait_ge(S["s_full"], t + 1)
                    V.tensor_copy(state[:, 2 * g:2 * g + 2, :], two(pb[T0])).then_inc(S["s_ev"], 1)
                if s == 2:
                    dve.wait_ge(S["ks_full"], t + 1)
                    V.tensor_tensor(r1[:, 2 * g:2 * g + 2, :],
                                    vtok[:, 4 * g:4 * g + 4, :].rearrange("p (s c) t -> p s c t", c=2)[:, :, 1, :],
                                    two(pb[T0]), ALU.subtract).then_inc(S["r1_made"], 1)
                gf = gate[:, 4 * g:4 * g + 4, :].rearrange("p u t -> p (u t)")
                if s == 4:
                    dve.wait_ge(S["o1_ev"], t + 1)
                    V.scalar_tensor_tensor(out=gf, in0=oT[:, 4 * g:4 * g + 4, :].rearrange("p u t -> p (u t)"),
                                           scalar=tw[:, C_ON:C_ON + 1], in1=gf,
                                           op0=ALU.mult, op1=ALU.mult).then_inc(S["gm_made"], 1)
                if s == 5:
                    dve.wait_ge(S["rno_made"], t + 1)
                    dve.wait_ge(S["gm_made"], t + 1)
                    V.tensor_tensor(gf, gf, sqo[:, g * HALF:(g + 1) * HALF], ALU.mult).then_inc(S["on_made"], 1)
                if s == 6:
                    for j in range(2):
                        dve.wait_ge(S["wo_full"], 2 * t + j + 1)
                        xv = x_res[:, 4 * g + 2 * j:4 * g + 2 * j + 2, :].rearrange("p n d -> p (n d)")
                        V.tensor_tensor(xv, xv, pb[(T0, T1)[j]][:, :], ALU.add).then_inc(S["wo_acc"], 1)

            def turn(h, hp, first, delta, prep):
                names = TURN if delta and prep else (NEXT if prep else OWN)
                base = turn_base(h) if delta else 0

                def conv(name):
                    z, hh = ("k", "q", "v").index(name[0]), int(name[1])
                    seqs = slice(2 * hh, 2 * hh + 2)
                    dve.wait_ge(S["pj_free"], base + (names.index(name) + 1))
                    for n, i in enumerate((2, 1, 0)):
                        if n:
                            dve.wait_ge(S["conv_tap"], 18 * hp + 6 * z + 3 * hh + n)
                        V.scalar_tensor_tensor(out=acc[:, z, seqs], in0=raw[:, z, seqs, i:i + T],
                                               scalar=hw[:, C_CONV + 4 * z + i:C_CONV + 4 * z + i + 1],
                                               in1=acc[:, z, seqs], op0=ALU.mult, op1=ALU.add).then_inc(S["conv_tap"], 1)

                for s in range(14):
                    g, l = s // LEVELS, s % LEVELS
                    if delta:
                        t = 2 * h + g
                        if l < LEVELS - 1:
                            mask(l + 1, g, t)
                        elif g == 0:
                            mask(0, 1, t + 1)
                        elif prep:
                            mask(0, 0, t + 1)
                        grow(l, g, t)
                        if not (first and g == 0):
                            tail(l, 1 - g, t - 1)
                        if s == 4:
                            set_up(h, 1, 2 * h + 1, first)
                    if not prep:
                        continue
                    for name in {1: ["k0"], 2: ["k1", "q0"], 3: ["q1"], 5: ["v0"], 6: ["v1"]}.get(s, []):
                        conv(name)
                    if s == 7:
                        dve.wait_ge(S["ea_made"], hp + 1)
                        V.tensor_scalar(nega[:, 1:2], nega[:, 0:1], -1.0, None, ALU.mult).then_inc(S["na_made"], 1)
                        dve.wait_ge(S["g_step"], 3 * hp + 3)
                        V.scalar_tensor_tensor(out=zg, in0=zg, scalar=0.0, in1=eg, op0=ALU.max,
                                               op1=ALU.add).then_inc(S["sp_made"], 1)
                    if s == 9:
                        dve.wait_ge(S["rn_made"], 2 * hp + 1)
                        V.tensor_tensor(qk[:, 0, :], kqs[:, 0, :], rn[:, 0, :], ALU.mult).then_inc(S["qk_made"], 1)
                    if s == 10:
                        dve.wait_ge(S["rn_made"], 2 * hp + 2)
                        V.scalar_tensor_tensor(out=qk[:, 1, :], in0=kqs[:, 1, :], scalar=float(P) ** -0.5,
                                               in1=rn[:, 1, :], op0=ALU.mult, op1=ALU.mult).then_inc(S["qk_made"], 1)
                    if s == 11:
                        if delta:
                            set_up(hp, 0, 2 * hp, False)
                        else:
                            set_up(0, 0, 0, True)

            turn(None, 0, False, False, True)
            mask(0, 0, 0)
            turn(0, 1, True, True, True)
            with dve.Fori(1, H - 1) as h:
                turn(h, h + 1, False, True, True)
            turn(H - 1, None, False, True, False)
            for s in range(LEVELS):
                tail(s, 1, 2 * H - 1)
            dve.wait_ge(S["wo_acc"], 4 * H)
            V.tensor_copy(lnv[:, 2, 0:1], x_res[:, 0, 0:1]).then_inc(S["attn_over"], 1)
            dve.wait_ge(S["attn_over"], 1)
            ffn(1)

        @block.tensor
        def _(pe):
            MM = nc.tensor.matmul
            pe.wait_ge(S["consts"], 6 + 2 * LEVELS)
            pe.wait_ge(S["consts_in"], 16)
            pe.wait_ge(S["onehot_made"], 1)

            def layernorm(k):
                for j in range(4):
                    pe.wait_ge(S["ln_xn"], NT * k + 2 * j + 2)
                    if j >= 2:
                        pe.wait_ge(S["ln_ev"], 4 * k + j - 1)
                    for n in range(2):
                        for kt in range(KT):
                            c = kt * 256 + n * P
                            last = nc.tensor.transpose(pb[j % 2][:, c:c + P],
                                                       (xn_attn if k == 1 else xn_ffn)[:, 2 * j + n, kt * P:(kt + 1) * P], ident[:, :])
                    last.then_inc(S["ln_tr"], 1)
                pe.wait_ge(S["ln_ev"], 4 * k + 4)

            def ffn(q):
                layernorm(2 * q)
                for n in range(NT):
                    for kt in range(KT):
                        last = MM(pb[7][:, n * NE:(n + 1) * NE], xnT[:, kt, n * P:(n + 1) * P],
                                  gwT[:, kt, :], start=kt == 0, stop=kt == KT - 1)
                last.then_inc(S["rt_logits"], 1)

                def shared(hh):
                    cols = slice(hh * HALF, (hh + 1) * HALF)
                    for m in range(3):
                        mw = min(P, ISH - m * P)
                        for u in range(2):
                            for kt in range(KT):
                                c = u * ISH + m * P
                                last = MM(pb[2 * m + u][0:mw, :], shw[:, kt, c:c + mw], xnT[:, kt, cols],
                                          start=kt == 0, stop=kt == KT - 1)
                            last.then_inc(S["sh_up" if u else "sh_gate"], 1)
                    pe.wait_ge(S["sh_h"], 6 * q + 3 * hh + 3)
                    for j in range(2):
                        if j == 1:
                            pe.wait_ge(S["rt_shift"], q + 1)
                        if hh:
                            pe.wait_ge(S["out_acc"], ACCS * q + j + 1)
                        for t in range(2):
                            for m in range(3):
                                mw = min(P, ISH - m * P)
                                c = (2 * j + t) * P
                                last = MM(pb[6 + j][:, t * D:(t + 1) * D], shh[m][0:mw, c:c + P],
                                          shd[0:mw, m, :], start=m == 0, stop=m == 2)
                        last.then_inc(S["sh_out"], 1)

                def turned(src, ready, made):
                    pe.wait_ge(ready, q + 1)
                    for j in range(2):
                        for t in range(4):
                            last = nc.tensor.transpose(pb[j][0:NE, t * P:(t + 1) * P], src[:, 4 * j + t, :],
                                                       ident[:, :])
                        last.then_inc(made, 1)

                pe.wait_ge(S["shared_in"], 32 * (q + 1))
                shared(0)
                turned(wd, S["rt_wd"], S["rt_wdt_tr"])
                pe.wait_ge(S["rt_wdt"], 2 * q + 2)
                for n in range(NT):
                    last = MM(pb[2][:, n * NE:(n + 1) * NE], wdT[:, n * P:(n + 1) * P], onehot[:, :],
                              start=True, stop=True)
                last.then_inc(S["rt_flat"], 1)
                pe.wait_ge(S["rt_mshift"], q + 1)
                shared(1)
                turned(soft.rearrange("p (n f) k -> p n (f k)", n=NT), S["rt_soft"], S["rt_soft_tr"])
                pe.wait_ge(S["soft_lo"], 2 * q + 2)

                def MM3(o, left, right, start, stop):
                    MM(o, left[1], right[0], start=start, stop=False)
                    MM(o, left[0], right[0], start=False, stop=False)
                    return MM(o, left[0], right[1], start=False, stop=stop)

                def both(pair, *at):
                    return pair[0][at], pair[1][at]

                ALL = slice(None)

                def front(g, gf, pf, par, fresh):
                    cols = slice(par * HALF, (par + 1) * HALF)
                    pe.wait_ge(S["r_lo"], gf + 1)
                    if not fresh:
                        pe.wait_ge(S["xe_made"], g)
                    for kt in range(KT):
                        last = MM3(pb[kt][:, :], both(rwr[pf], ALL, slice(kt * P, (kt + 1) * P)),
                                   both(softT, ALL, cols), True, True)
                    last.then_inc(S["x_full"], 1)
                    if not fresh:
                        pe.wait_ge(S["we_ev"], g)
                    MM(pb[2][:, :], rwr[pf][0][:, 256:384], softT[0][:, cols], start=True, stop=False)
                    MM(pb[2][:, :], rwr[pf][0][:, 256:384], softT[1][:, cols], start=False,
                       stop=True).then_inc(S["we_full"], 1)

                def low_rank(g, gf, pf, par, fresh):
                    pe.wait_ge(S["xe_lo"], g + 1)
                    pe.wait_ge(S["w_lo"], 3 * gf + 3)
                    if not fresh:
                        pe.wait_ge(S["aw_made"], g)
                    for kt in range(KT):
                        c = C_QA + kt * P
                        last = MM3(pb[3][:, :], both(ewr[pf], ALL, slice(c, c + P)),
                                   both(xer[par], ALL, kt, ALL), kt == 0, kt == KT - 1)
                    last.then_inc(S["a_made"], 1)

                def inner(t, pf, par):
                    for kt in range(KT):
                        c = C_GU + kt * 384 + t * P
                        MM3(pb[4 + t][:, :], both(ewr[pf], ALL, slice(c, c + P)),
                            both(xer[par], ALL, kt, ALL), kt == 0, False)

                def step(g, gf, j, first, left):
                    pf, hh = j // 2, j % 2
                    if first:
                        pe.wait_ge(S["out_acc"], 2 * g + 4 * (q + 1))
                    else:
                        pe.wait_ge(S["out_acc"], 2 * g + 4 * (q + 1) - 1)
                    inner(1, pf, hh)
                    if not first:
                        pe.wait_ge(S["out_acc"], 2 * g + 4 * (q + 1))
                    inner(2, pf, hh)
                    pe.wait_ge(S["aw_lo"], g + 1)
                    for t in range(3):
                        c = C_QB + t * P
                        MM3(pb[4 + t][:, :], both(ewr[pf], ALL, slice(c, c + P)), both(awr, ALL, ALL),
                            False, True).then_inc(S["gu_full"], 1)
                    if left > 2:
                        front(g + 2, gf + 1, 1 - pf, hh, False)
                    if left > 1:
                        low_rank(g + 1, gf + hh, (1 - pf) if hh else pf, 1 - hh, False)
                    pe.wait_ge(S["h_lo"], 3 * g + 2)
                    MM3(pb[7][:, :], both(ewr[pf], ALL, slice(C_DQ, C_DQ + P)), both(h1r[hh], ALL, ALL), True, False)
                    MM3(pb[7][:, :], both(ewr[pf], slice(0, IR), slice(C_DQ + P, C_DQ + 2 * P)),
                        both(h2r[hh], slice(0, IR), ALL), False, True).then_inc(S["da_full"], 1)
                    if left > 1:
                        inner(0, (1 - pf) if hh else pf, 1 - hh)
                    pe.wait_ge(S["h_lo"], 3 * g + 3)
                    for k in range(2):
                        for t in range(2):
                            c = (2 * k + t) * P
                            o = pb[5 + k][:, t * D:(t + 1) * D]
                            MM3(o, both(h1r[hh], ALL, slice(c, c + P)), both(ewr[pf], ALL, slice(C_D1, C_D2)), True, False)
                            last = MM3(o, both(h2r[hh], ALL, slice(c, c + P)), both(ewr[pf], ALL, slice(C_D2, C_DQ)),
                                       False, True)
                        last.then_inc(S["out_full"], 1)

                front(STEPS * q, F * q, 0, 0, q == 0)
                front(STEPS * q + 1, F * q, 0, 1, False)
                low_rank(STEPS * q, F * q, 0, 0, q == 0)
                inner(0, 0, 0)
                with pe.Fori(0, F // 2 - 1) as i:
                    for j in range(4):
                        step(4 * i + (STEPS * q + j), 2 * i + (F * q + j // 2), j, j == 0, STEPS)
                for j in range(4):
                    step(STEPS * (q + 1) - 4 + j, F * (q + 1) - 2 + j // 2, j, False, 4 - j)

            ffn(0)
            pe.wait_ge(S["ffn_over"], 1)
            layernorm(1)
            pe.wait_ge(S["attn_in"], 32)
            for n in range(NT):
                for kt in range(KT):
                    last = MM(pb[4][:, n * H:(n + 1) * H], xnT[:, kt, n * P:(n + 1) * P], wbs[:, kt, :],
                              start=kt == 0, stop=kt == KT - 1)
            last.then_inc(S["beta_full"], 1)
            for hh in range(2):
                for kt in range(KT):
                    last = MM(pb[5 + hh][:, :], wf1s[:, kt, :], xnT[:, kt, hh * HALF:(hh + 1) * HALF],
                              start=kt == 0, stop=kt == KT - 1)
                last.then_inc(S["xf_full"], 1)
            pe.wait_ge(S["xf_ev"], 2)
            pe.wait_ge(S["beta_made"], 1)

            def decayed(l, g, t, fresh):
                m = 1 << l
                if l == 0:
                    pe.wait_ge(S["kr_set"], t + 1)
                else:
                    pe.wait_ge(S["lvl_upd"], 14 * t + 2 * l)
                if not (fresh and l < 2):
                    pe.wait_ge(S["masked"], 14 * t + (2 * l - 2))
                for u in range(4):
                    rhs = kq[:, :, 4 * g + u, :].rearrange("p z (n s m) -> p z n s m", s=2, m=m)[:, :, :, 1, :]
                    last = MM(pb[(l + g) % 2][:, u * P:(u + 1) * P].rearrange("p (z n m) -> p z n m", z=2, m=m),
                              kr[:, 4 * g + u, :], rhs, start=True, stop=True)
                last.then_inc(S["al_full"], 1)

            def product(l, g, t, fresh):
                m = 1 << l
                pe.wait_ge(S["masked"], 14 * t + 2 * l + 1)
                if l == 0:
                    pe.wait_ge(S["vw_set"], t + 1)
                else:
                    pe.wait_ge(S["vw_upd"], 13 * t + (2 * l - 1))
                if not (fresh and l == 0):
                    pe.wait_ge(S["p_ev"], 7 * t + l)
                for u in range(4):
                    last = MM(pb[2][:, u * 64:(u + 1) * 64].rearrange("p (n m) -> p n m", m=m),
                              bt[l][:, 4 * g + u, :], halves(vw[:, 1, 4 * g + u, :], m, 0), start=True, stop=True)
                last.then_inc(S["p_full"], 1)

            def growth(l, g, t, fresh):
                m = 1 << l
                if not (fresh and l == 0):
                    pe.wait_ge(S["vw_upd"], 13 * t + 2 * l)
                pe.wait_ge(S["p_ev"], 7 * t + l + 1)
                for u in range(4):
                    n = 4 * g + u
                    last = MM(pb[3][:, u * 64:(u + 1) * 64].rearrange("p (n m) -> p n m", m=m),
                              pt[l][:, n, :], halves(vw[:, 0, n, :], m, 1), start=True, stop=True)
                    if l < LEVELS - 1:
                        last = MM(pb[3][:, 256 + u * 64:256 + (u + 1) * 64].rearrange("p (n m) -> p n m", m=m),
                                  vw[:, 0, n, :], halves(pt[l][:, n, :], m, 0), start=True, stop=True)
                last.then_inc(S["d_full"], 1)

            def tail(s, g, t, vt_done, fresh):
                def cols(bank, b):
                    return bank[:, b * P:(b + 1) * P]

                pair = ((0, 4 * g), (1, 4 * g + 2))
                if s == 0:
                    pe.wait_ge(S["vw_upd"], 13 * t + 13)
                    pe.wait_ge(S["pj_free"], vt_done)
                    if not fresh:
                        pe.wait_ge(S["wo_acc"], 2 * t)
                    for b, n in pair:
                        last = MM(cols(pb[T0], b), vw[:, 0, n, :], vtok[:, n, :], start=True, stop=True)
                    last.then_inc(S["u0_full"], 1)
                    pe.wait_ge(S["lvl_upd"], 14 * t + 14)
                    for b, n in pair:
                        last = nc.tensor.transpose(cols(pb[T1], b), kr[:, n, :], ident[:, :])
                    last.then_inc(S["krt_full"], 1)
                if s == 1:
                    pe.wait_ge(S["u0_ev"], t + 1)
                    pe.wait_ge(S["krt_ev"], t + 1)
                    for b, n in pair:
                        last = MM(cols(pb[T0], b), krt[:, 2 * g + b, :], uu[:, n, :], start=True, stop=True)
                    last.then_inc(S["s_full"], 1)
                    pe.wait_ge(S["masked"], 14 * t + 14)
                    for b, n in pair:
                        last = MM(cols(pb[T1], b), uu[:, n, :], aq[:, n, :], start=True, stop=True)
                    last.then_inc(S["o0_full"], 1)
                if s == 2:
                    pe.wait_ge(S["s_ev"], t + 1)
                    for b, n in pair:
                        last = MM(cols(pb[T0], b), kq[:, 0, n + 1, :], state[:, 2 * g + b, :], start=True, stop=True)
                    last.then_inc(S["ks_full"], 1)
                if s == 3:
                    pe.wait_ge(S["r1_made"], t + 1)
                    pe.wait_ge(S["o0_ev"], t + 1)
                    for b, n in pair:
                        last = MM(cols(pb[T1], b), vw[:, 0, n + 1, :], r1[:, 2 * g + b, :], start=True, stop=True)
                    last.then_inc(S["u1_full"], 1)
                if s == 4:
                    pe.wait_ge(S["u1_ev"], t + 1)
                    for b, n in pair:
                        MM(cols(pb[T0], b), state[:, 2 * g + b, :], kq[:, 1, n + 1, :], start=True, stop=False)
                        last = MM(cols(pb[T0], b), uu[:, n + 1, :], aq[:, n + 1, :], start=False, stop=True)
                    last.then_inc(S["o1_full"], 1)
                if s == 5:
                    pe.wait_ge(S["sqo_made"], t + 1)
                    MM(pb[T1][:, :], ones[:, :], sqo[:, g * HALF:(g + 1) * HALF], start=True,
                       stop=True).then_inc(S["n_full"], 1)
                if s == 6:
                    pe.wait_ge(S["on_made"], t + 1)
                    for j in range(2):
                        for i in range(2):
                            last = MM(pb[(T0, T1)[j]][:, i * D:(i + 1) * D], gate[:, 4 * g + 2 * j + i, :],
                                      tw[:, C_WO:C_WO + D], start=True, stop=True)
                        last.then_inc(S["wo_full"], 1)

            def turn(h, hp, first, delta, prep):
                names = TURN if delta and prep else (NEXT if prep else OWN)
                base = turn_base(h) if delta else 0

                def item(name):
                    n = names.index(name)
                    kind, hh = name[:-1], int(name[-1])
                    cols = slice(hh * HALF, (hh + 1) * HALF)
                    bank = pb[5 + n % 2]
                    if delta or n >= 2:
                        pe.wait_ge(S["pj_free"], base + (n - 1))
                    if kind in ("k", "q", "v"):
                        z = ("k", "q", "v").index(kind)
                        if name == "k0":
                            pe.wait_ge(S["head_in"], 16 * hp + 16)
                        for kt in range(KT):
                            c = C_KQV + kt * 384 + z * P
                            last = MM(bank[:, :], hw[:, c:c + P], xnT[:, kt, cols], start=kt == 0, stop=kt == KT - 1)
                    elif kind == "g":
                        last = MM(bank[:, :], hw[:, C_F2:C_F2 + P], xfT[:, cols], start=True, stop=True)
                    elif kind == "gt":
                        pe.wait_ge(S["tail_in"], 16 * h + 16)
                        for kt in range(KT):
                            last = MM(bank[:, :], tw[:, C_G + kt * P:C_G + (kt + 1) * P], xnT[:, kt, cols],
                                      start=kt == 0, stop=kt == KT - 1)
                    elif kind == "vt":
                        pe.wait_ge(S["silu_head"], 3 * h + 3)
                        for u in range(4):
                            c = (4 * hh + u) * P
                            last = nc.tensor.transpose(bank[:, u * P:(u + 1) * P], vs[:, c:c + P], ident[:, :])
                    elif kind in ("sk", "sq"):
                        z = ("sk", "sq").index(kind)
                        pe.wait_ge(S["sq_head"], 2 * hp + z + 1)
                        last = MM(bank[:, :], ones[:, :], acc[:, z].rearrange("p s t -> p (s t)")[:, cols],
                                  start=True, stop=True)
                    else:
                        pe.wait_ge(S["prod_made"], hp + 1)
                        for u in range(4):
                            c = (4 * hh + u) * P
                            last = MM(bank[:, u * 64:(u + 1) * 64], prod[:, c:c + P], ones[:, 0:64], start=True,
                                      stop=True)
                    last.then_inc(S["pj_full"], 1)

                for s in range(14):
                    g, l = s // LEVELS, s % LEVELS
                    if delta:
                        t = 2 * h + g
                        product(l, g, t, first and g == 0)
                        if l < LEVELS - 1:
                            decayed(l + 1, g, t, first and g == 0)
                        elif g == 0:
                            decayed(0, 1, t + 1, False)
                        elif prep:
                            decayed(0, 0, t + 1, False)
                    for name in BEFORE[s]:
                        if name in names:
                            item(name)
                    if delta:
                        growth(l, g, t, first and g == 0)
                        if g == 1:
                            tail(l, 0, t - 1, own("vt0", h, not prep), first)
                        elif not first:
                            tail(l, 1, t - 1, own("vt1", h - 1, False), False)
                    for name in AFTER[s]:
                        if name in names:
                            item(name)

            turn(None, 0, False, False, True)
            decayed(0, 0, 0, True)
            turn(0, 1, True, True, True)
            with pe.Fori(1, H - 1) as h:
                turn(h, h + 1, False, True, True)
            turn(H - 1, None, False, True, False)
            for s in range(LEVELS):
                tail(s, 1, 2 * H - 1, own("vt1", H - 1, True), False)
            pe.wait_ge(S["attn_over"], 1)
            ffn(1)


def kernel(**inputs):
    import numpy as np
    import concourse.bacc as bacc
    from concourse.bass_utils import run_bass_kernel_spmd

    a = {n: np.asarray(v) for n, v in inputs.items()}
    f = {n[len("L0_ffn_"):]: v for n, v in a.items() if n.startswith("L0_ffn_")}
    t = {n[len("L0_attn_"):]: v for n, v in a.items() if n.startswith("L0_attn_")}

    def tiles(w):
        return w.reshape(-1, P, w.shape[1]).transpose(1, 0, 2)

    ew = np.zeros((F, P, C_EW), np.float32)
    es = np.zeros((F, 640), np.float32)
    rw = np.zeros((F, NE, 384), np.float32)
    for g in range(F):
        gu = np.zeros((P, KT, 384), np.float32)
        for c, n in ((0, "gate_W"), (1, "up_W")):
            w = tiles(f[n][g].T)
            gu[:, :, c * P:(c + 1) * P] = w[:, :, 0:P]
            gu[:, :, 256 + 64 * c:256 + 64 * c + IR] = w[:, :, P:I]
        ew[g, :, C_GU:C_QA] = gu.reshape(P, 768)
        qa = np.zeros((P, KT, P), np.float32)
        for c, n in ((0, "gate"), (1, "up")):
            qa[:, :, 64 * c:64 * c + 64] = tiles(f[n + "_qa"][g].reshape(KR, D).T)
            qb = f[n + "_qb"][g].transpose(0, 2, 1).reshape(KR, I)
            rows = slice(64 * c, 64 * c + 64)
            ew[g, rows, C_QB + c * P:C_QB + (c + 1) * P] = qb[:, 0:P]
            ew[g, rows, C_QB + 256 + 64 * c:C_QB + 256 + 64 * c + IR] = qb[:, P:I]
            es[g, c * P:(c + 1) * P] = f[n + "_scale"][g, 0:P]
            es[g, 256 + 64 * c:256 + 64 * c + IR] = f[n + "_scale"][g, P:I]
        ew[g, :, C_QA:C_QB] = qa.reshape(P, 256)
        down = f["down_W"][g].T
        ew[g, :, C_D1:C_D2] = down[0:P]
        ew[g, 0:IR, C_D2:C_DQ] = down[P:I]
        ew[g, 64:P, C_D2:C_DQ] = f["down_qb"][g].transpose(0, 2, 1).reshape(KR, D)
        dq = f["down_qa"][g].reshape(KR, I).T
        ew[g, :, C_DQ + 64:C_DQ + P] = dq[0:P]
        ew[g, 0:IR, C_DQ + P + 64:C_DQ + 2 * P] = dq[P:I]
        es[g, 384:640] = f["down_scale"][g]
        rw[g, g * K8:(g + 1) * K8, 0:D] = f["mask_up_W"][g].T
        for c in range(2):
            for k in range(K8):
                rw[g, g * K8 + k, 256 + 64 * c + k * R:256 + 64 * c + (k + 1) * R] = 1.0
    sgu = np.ascontiguousarray(tiles(np.concatenate([f["sh_gate_W"].T, f["sh_up_W"].T], 1)))
    sdn = np.zeros((3 * P, D), np.float32)
    sdn[0:ISH] = f["sh_down_W"].T
    sdn = np.ascontiguousarray(tiles(sdn))

    hw = np.zeros((H, P, C_HW), np.float32)
    tw = np.zeros((H, P, C_TW), np.float32)
    for h in range(H):
        cols = slice(h * P, (h + 1) * P)
        for z, n in enumerate("kqv"):
            w = tiles(t["W" + n][:, cols])
            for kt in range(KT):
                hw[h, :, kt * 384 + z * P:kt * 384 + (z + 1) * P] = w[:, kt]
            hw[h, :, C_CONV + 4 * z:C_CONV + 4 * z + 4] = t["conv_" + n][cols]
        hw[h, :, C_F2:C_F2 + P] = t["Wf2"][:, cols]
        hw[h, :, C_DT] = t["dt_bias"][cols]
        hw[h, :, C_AL] = t["A_log"][h]
        tw[h, :, C_G:C_WO] = tiles(t["Wg"][:, cols]).reshape(P, 256)
        tw[h, :, C_WO:C_BG] = t["Wo"][cols]
        tw[h, :, C_BG] = t["bg"][cols]
        tw[h, :, C_ON] = t["o_norm_w"]

    arrays = {
        "x": np.ascontiguousarray(t["hidden_states"].reshape(NT, P, D)),
        "gate_wT": np.ascontiguousarray(tiles(f["gate_weight"].T)),
        "expert_w": ew, "expert_scale": es, "route_w": rw, "shared_gu": sgu, "shared_down": sdn,
        "inv_map": np.ascontiguousarray(f["inv_mapping"].reshape(NE)),
        "head_w": hw, "tail_w": tw,
        "wf1": np.ascontiguousarray(tiles(t["Wf1"])),
        "wb": np.ascontiguousarray(tiles(t["Wb"])),
    }
    nc = bacc.Bacc("TRN2", target_bir_lowering=False, num_devices=1)
    args = [nc.dram_tensor(n, v.shape, mybir.dt.from_np(v.dtype), kind="ExternalInput").ap()
            for n, v in arrays.items()]
    out = nc.dram_tensor("out", (NT, P, D), mybir.dt.float32, kind="ExternalOutput").ap()
    macaron_kernel(nc, *args, out)
    r = run_bass_kernel_spmd(nc, [arrays], core_ids=[0])
    return r.results[0]["out"].reshape(NSEQ, T, D)
```
